# Optimizing a Trainium2 kernel written in Bass

```python
import numpy as np
import jax
import jax.numpy as jnp

def _softmax(x, axis=-1):
    return jax.nn.softmax(x, axis=axis)

def _gelu(x):
    return jax.nn.gelu(x, approximate=True)

def _silu(x):
    return jax.nn.silu(x)

def _sigmoid(x):
    return jax.nn.sigmoid(x)

def _layernorm(x, axis=-1, eps=1e-05):
    m = jnp.mean(x, axis=axis, keepdims=True)
    v = jnp.var(x, axis=axis, keepdims=True)
    return (x - m) / jnp.sqrt(v + eps)

def _scatter_add(tgt, idx, src, axis=0):
    return tgt.at[idx].add(src)

def _segment_sum(src, seg, n):
    return jax.ops.segment_sum(src, seg, n)
kernel_name = 'mk_decoder_postln_d1_seqx_r8_0ee990'

def setup_inputs(seed: int=0):
    np.random.seed(seed)
    _w = jnp.asarray

    def _rec_inputs():
        import jax
        import jax.numpy as jnp
        _rk = jax.random.key(seed)
        x = -0.0003929 + 0.9999 * jax.random.normal(jax.random.fold_in(_rk, 1), (8, 128, 128), jnp.float32)
        _lenS = 128 - jax.random.randint(jax.random.fold_in(_rk, 7), (8,), 0, max(1, 128 // 4) + 1, jnp.int32)
        _lenS2 = 77 - jax.random.randint(jax.random.fold_in(_rk, 8), (8,), 0, max(1, 77 // 4) + 1, jnp.int32)
        _ctx_1024P = jax.random.normal(jax.random.fold_in(_rk, 11), (8, 16, 128), jnp.float32)
        _ctx_1024c = jax.random.dirichlet(jax.random.fold_in(_rk, 511), 0.3 * jnp.ones((16,), jnp.float32), (8, 77))
        _ctx_1024t = jnp.einsum('bsk,bkd->bsd', _ctx_1024c, _ctx_1024P)
        _ctx_1024t = _ctx_1024t * jax.lax.rsqrt(jnp.mean(jnp.square(_ctx_1024t)) + 1e-12) * 0.953939
        ctx_1024 = 4.13588e-05 + 0.999923 * (_ctx_1024t + 0.3 * jax.random.normal(jax.random.fold_in(_rk, 611), (8, 77, 128), jnp.float32))
        return (x, ctx_1024)
    x, ctx_1024 = _rec_inputs()

    def _L0_attn_setup():
        import jax, jax.numpy as jnp
        import numpy as np
        import math
        D_MODEL = 128
        NUM_HEADS = 16
        D_HEAD = D_MODEL // NUM_HEADS
        B, T = (8, 128)

        def rel_pos_encoding(seq_len, d, dtype=jnp.float32):
            pos = jnp.arange(seq_len, dtype=jnp.float32)[:, None]
            div = jnp.exp(jnp.arange(0, d, 2, dtype=jnp.float32) * (-math.log(10000.0) / d))
            ang = pos * div
            pe_pos = jnp.stack([jnp.sin(ang), jnp.cos(ang)], axis=-1).reshape(seq_len, d)
            pe_neg = jnp.stack([jnp.sin(-ang), jnp.cos(-ang)], axis=-1).reshape(seq_len, d)
            pe = jnp.concatenate([pe_pos[::-1], pe_neg[1:]], axis=0)
            return pe.astype(dtype)

        def _rel_shift(pos_score):
            b, h, t1, t2 = pos_score.shape
            padded = jnp.pad(pos_score, ((0, 0), (0, 0), (0, 0), (1, 0)))
            padded = padded.reshape(b, h, t2 + 1, t1)
            return padded[:, :, 1:].reshape(b, h, t1, t2)[:, :, :, :t1]
        key = jax.random.key(seed)
        ks = jax.random.split(key, 9)
        D = D_MODEL
        s = 1.0 / math.sqrt(D)
        return {'x': jax.random.normal(ks[0], (B, T, D), jnp.float32), 'Wq': jax.random.normal(ks[1], (D, D), jnp.float32) * s, 'bq': jnp.zeros((D,), jnp.float32), 'Wk': jax.random.normal(ks[2], (D, D), jnp.float32) * s, 'bk': jnp.zeros((D,), jnp.float32), 'Wv': jax.random.normal(ks[3], (D, D), jnp.float32) * s, 'bv': jnp.zeros((D,), jnp.float32), 'Wpos': jax.random.normal(ks[4], (D, D), jnp.float32) * s, 'Wout': jax.random.normal(ks[5], (D, D), jnp.float32) * s, 'bout': jnp.zeros((D,), jnp.float32), 'u_bias': jax.random.normal(ks[6], (NUM_HEADS, D_HEAD), jnp.float32) * 0.1, 'v_bias': jax.random.normal(ks[7], (NUM_HEADS, D_HEAD), jnp.float32) * 0.1, 'ln_gamma': jnp.ones((D,), jnp.float32), 'ln_beta': jnp.zeros((D,), jnp.float32)}
    _L0_attn_all = _L0_attn_setup()
    _L0_attn_in = {k: v for k, v in _L0_attn_all.items() if k in ('Wq', 'bq', 'Wk', 'bk', 'Wv', 'bv', 'Wpos', 'Wout', 'bout', 'u_bias', 'v_bias', 'ln_gamma', 'ln_beta')}
    del _L0_attn_all

    def _L0_xattn_setup():
        import jax, jax.numpy as jnp
        import numpy as np
        key = jax.random.key(seed)
        k1, k2 = jax.random.split(key)
        B, L, V, D = (8, 256, 128, 128)
        hidden_states = jax.random.normal(k1, (B, L, D), dtype=jnp.float32)
        visual_hidden_state = jax.random.normal(k2, (B, V, D), dtype=jnp.float32)
        return {'hidden_states': hidden_states, 'visual_hidden_state': visual_hidden_state}
    _L0_xattn_all = _L0_xattn_setup()
    _L0_xattn_in = {k: v for k, v in _L0_xattn_all.items() if k in ()}
    del _L0_xattn_all

    def _L0_ffn_setup():
        import jax, jax.numpy as jnp
        import numpy as np
        B, S, D = (2, 256, 128)
        E, K, F = (16, 2, 64)
        FS = 128
        key = jax.random.key(seed)
        ks = jax.random.split(key, 8)

        def w(k, shape, fan_in):
            return jax.random.normal(k, shape, jnp.float32) / np.sqrt(fan_in).astype(np.float32)
        return {'x': jax.random.normal(ks[0], (B, S, D), jnp.float32), 'Wr': w(ks[1], (D, E), D), 'Wg': w(ks[2], (E, D, F), D), 'Wu': w(ks[3], (E, D, F), D), 'Wd': w(ks[4], (E, F, D), F), 'Sg': w(ks[5], (D, FS), D), 'Su': w(ks[6], (D, FS), D), 'Sd': w(ks[7], (FS, D), FS)}
    _L0_ffn_all = _L0_ffn_setup()
    _L0_ffn_in = {k: v for k, v in _L0_ffn_all.items() if k in ('Wr', 'Wg', 'Wu', 'Wd', 'Sg', 'Su', 'Sd')}
    del _L0_ffn_all
    return {'x': x, 'ctx_1024': ctx_1024, 'L0_attn_Wq': _L0_attn_in['Wq'], 'L0_attn_bq': _L0_attn_in['bq'], 'L0_attn_Wk': _L0_attn_in['Wk'], 'L0_attn_bk': _L0_attn_in['bk'], 'L0_attn_Wv': _L0_attn_in['Wv'], 'L0_attn_bv': _L0_attn_in['bv'], 'L0_attn_Wpos': _L0_attn_in['Wpos'], 'L0_attn_Wout': _L0_attn_in['Wout'], 'L0_attn_bout': _L0_attn_in['bout'], 'L0_attn_u_bias': _L0_attn_in['u_bias'], 'L0_attn_v_bias': _L0_attn_in['v_bias'], 'L0_attn_ln_gamma': _L0_attn_in['ln_gamma'], 'L0_attn_ln_beta': _L0_attn_in['ln_beta'], 'L0_ffn_Wr': _L0_ffn_in['Wr'], 'L0_ffn_Wg': _L0_ffn_in['Wg'], 'L0_ffn_Wu': _L0_ffn_in['Wu'], 'L0_ffn_Wd': _L0_ffn_in['Wd'], 'L0_ffn_Sg': _L0_ffn_in['Sg'], 'L0_ffn_Su': _L0_ffn_in['Su'], 'L0_ffn_Sd': _L0_ffn_in['Sd']}

def reference(x, ctx_1024, L0_attn_Wq, L0_attn_bq, L0_attn_Wk, L0_attn_bk, L0_attn_Wv, L0_attn_bv, L0_attn_Wpos, L0_attn_Wout, L0_attn_bout, L0_attn_u_bias, L0_attn_v_bias, L0_attn_ln_gamma, L0_attn_ln_beta, L0_ffn_Wr, L0_ffn_Wg, L0_ffn_Wu, L0_ffn_Wd, L0_ffn_Sg, L0_ffn_Su, L0_ffn_Sd):
    import jax
    import jax.numpy as jnp

    def _L0_attn_ref(x, Wq, bq, Wk, bk, Wv, bv, Wpos, Wout, bout, u_bias, v_bias, ln_gamma, ln_beta):
        import jax, jax.numpy as jnp
        import numpy as np
        import math
        D_MODEL = 128
        NUM_HEADS = 16
        D_HEAD = D_MODEL // NUM_HEADS
        B, T = (8, 128)

        def rel_pos_encoding(seq_len, d, dtype=jnp.float32):
            pos = jnp.arange(seq_len, dtype=jnp.float32)[:, None]
            div = jnp.exp(jnp.arange(0, d, 2, dtype=jnp.float32) * (-math.log(10000.0) / d))
            ang = pos * div
            pe_pos = jnp.stack([jnp.sin(ang), jnp.cos(ang)], axis=-1).reshape(seq_len, d)
            pe_neg = jnp.stack([jnp.sin(-ang), jnp.cos(-ang)], axis=-1).reshape(seq_len, d)
            pe = jnp.concatenate([pe_pos[::-1], pe_neg[1:]], axis=0)
            return pe.astype(dtype)

        def _rel_shift(pos_score):
            b, h, t1, t2 = pos_score.shape
            padded = jnp.pad(pos_score, ((0, 0), (0, 0), (0, 0), (1, 0)))
            padded = padded.reshape(b, h, t2 + 1, t1)
            return padded[:, :, 1:].reshape(b, h, t1, t2)[:, :, :, :t1]
        b, t, d = x.shape
        h, dh = (NUM_HEADS, D_HEAD)
        mu = jnp.mean(x, axis=-1, keepdims=True)
        var = jnp.mean((x - mu) ** 2, axis=-1, keepdims=True)
        xn = (x - mu) * jax.lax.rsqrt(var + 1e-05) * ln_gamma + ln_beta
        pos_emb = rel_pos_encoding(t, d, x.dtype)
        q = (xn @ Wq.T + bq).reshape(b, t, h, dh)
        k = (xn @ Wk.T + bk).reshape(b, t, h, dh)
        v = (xn @ Wv.T + bv).reshape(b, t, h, dh)
        p = (pos_emb @ Wpos.T).reshape(2 * t - 1, h, dh)
        content_score = jnp.einsum('bthd,bshd->bhts', q + u_bias, k)
        pos_score = jnp.einsum('bthd,phd->bhtp', q + v_bias, p)
        pos_score = _rel_shift(pos_score)
        score = (content_score + pos_score) / math.sqrt(dh)
        attn = jax.nn.softmax(score, axis=-1)
        ctx = jnp.einsum('bhts,bshd->bthd', attn, v).reshape(b, t, d)
        return ctx @ Wout.T + bout

    def _L0_xattn_ref(hidden_states, visual_hidden_state):
        import jax, jax.numpy as jnp
        import numpy as np
        scores = jnp.einsum('bld,bvd->blv', hidden_states, visual_hidden_state)
        probs = jax.nn.softmax(scores, axis=-1)
        return jnp.einsum('blv,bvd->bld', probs, visual_hidden_state)

    def _L0_ffn_ref(x, Wr, Wg, Wu, Wd, Sg, Su, Sd):
        import jax, jax.numpy as jnp
        import numpy as np
        B, S, D = (2, 256, 128)
        E, K, F = (16, 2, 64)
        FS = 128
        b, s, d = x.shape
        T = b * s
        xf = x.reshape(T, d)
        shared = jax.nn.silu(xf @ Sg) * (xf @ Su) @ Sd
        probs = jax.nn.softmax(xf @ Wr, axis=-1)
        topk_p, topk_i = jax.lax.top_k(probs, K)
        n_exp = Wr.shape[1]
        cw = jnp.zeros((T, n_exp), x.dtype).at[jnp.arange(T)[:, None], topk_i].add(topk_p)

        def step(acc, ew):
            wg, wu, wd, c = ew
            y = jax.nn.silu(xf @ wg) * (xf @ wu) @ wd
            return (acc + y * c[:, None], None)
        routed, _ = jax.lax.scan(step, jnp.zeros_like(xf), (Wg, Wu, Wd, cw.T))
        return (routed + shared).reshape(b, s, d)
    x = _layernorm(x + _L0_attn_ref(x, L0_attn_Wq, L0_attn_bq, L0_attn_Wk, L0_attn_bk, L0_attn_Wv, L0_attn_bv, L0_attn_Wpos, L0_attn_Wout, L0_attn_bout, L0_attn_u_bias, L0_attn_v_bias, L0_attn_ln_gamma, L0_attn_ln_beta), axis=-1)
    x = _layernorm(x + _L0_xattn_ref(x, ctx_1024), axis=-1)
    x = _layernorm(x + _L0_ffn_ref(x, L0_ffn_Wr, L0_ffn_Wg, L0_ffn_Wu, L0_ffn_Wd, L0_ffn_Sg, L0_ffn_Su, L0_ffn_Sd), axis=-1)
    return x

_drawn_inputs = setup_inputs


def setup_inputs(seed=0):
    import zlib

    import numpy as np

    out = dict(_drawn_inputs(seed))
    spreads = {'L0_attn_bq': (0.0, 0.1),
     'L0_attn_bk': (0.0, 0.8),
     'L0_attn_bv': (0.0, 0.1),
     'L0_attn_bout': (0.0, 0.1),
     'L0_attn_ln_gamma': (1.0, 0.2),
     'L0_attn_ln_beta': (0.0, 0.1)}
    factors = {'L0_attn_v_bias': 2.763}
    for name, (base, spread) in spreads.items():
        noise = np.random.default_rng([zlib.crc32(name.encode()), seed]).standard_normal(out[name].shape)
        drawn = base * np.exp(spread * noise) if base else spread * noise
        out[name] = jnp.asarray(drawn.astype(out[name].dtype))
    for name, factor in factors.items():
        out[name] = (out[name] * factor).astype(out[name].dtype)
    return out
```

```python
from contextlib import ExitStack

import concourse.bass as bass
from concourse import mybir

P = 128
ALU = mybir.AluOpType
ACT = mybir.ActivationFunctionType
AX = mybir.AxisListType.X
F32 = mybir.dt.float32
F32R = mybir.dt.float32r
F16 = mybir.dt.float16
BF16 = mybir.dt.bfloat16
U32 = mybir.dt.uint32

B, T, D = 8, 128, 128
S = 77
H, DH = 16, 8
E, F = 16, 64
HG = 4
NG = H // HG
PARTS = 4
POS = 2 * T
KPT = B * T + POS
CI = 16
NCH = T // CI
UNITS = 2 * NCH
UCOL = 2 * 512
BLK = 32
NBLK = UCOL // BLK
G = 2
GB = B // G
GT = GB * T
PAIRS = E // 2
HID = PAIRS + 1
EPS = 1e-5
VW = 2 * DH + 1
SC = DH ** -0.5
BIG = 1e30
SHARED = PAIRS
NK = G * HID



def decoder_block(nc, x, ctx_n, ctx_t, w_proj, w_r, w_ffn, w_down, cols, rows, pos_emb, ident_d, sel_d, tie_d, out):
    es = ExitStack()
    with es:
        def sb(name, shape, dt):
            return es.enter_context(nc.sbuf_tensor(name, shape, dt))

        def sem(name):
            return es.enter_context(nc.semaphore(name))

        ps = es.enter_context(nc.psum_tensor("ps", [P, 8, 512], F32))
        kp_scr = nc.dram_tensor("kp_scr", (HG, PARTS, DH, NG, KPT), F16, kind="Internal").ap()
        q_scr = nc.dram_tensor("q_scr", (HG, PARTS, DH, NG, 2, B * T), F16, kind="Internal").ap()

        x_sb = sb("x_sb", [P, B, D], F32)
        wp = sb("wp", [P, 5, D], F32)
        wr = sb("wr", [P, E], F32)
        cl = sb("cl", [P, 6], F32)
        rw = sb("rw", [P, 2, D], F32)
        pe_sb = sb("pe_sb", [P, POS], F32)
        ident = sb("ident", [P, P], F32)

        st = sb("st", [P, B, 6], F32)
        mv = sb("mv", [P, B, 2], F32)
        ve = sb("ve", [P, B], F32)
        half = sb("half", [P, B], F32)
        rstd = sb("rstd", [P, B], F32)
        xh = sb("xh", [P, B, D], F32)
        v32 = xh
        xnT = sb("xnT", [P, B * T], F32)
        x2T = xnT
        qb = sb("qb", [P, 2], F32)
        kp_c = sb("kp_c", [P, 2, KPT], F16)
        q_c = sb("q_c", [P, 2, 2, B * T], F16)
        p32 = q_c[:, :, :, :].rearrange("p a s t -> p a (s t)").bitcast(F32)
        kp = sb("kp", [P, NG, KPT], F16)
        qd = sb("qd", [P, NG, 2, HG, B * T], F16)
        vp = sb("vp", [P, B, H, VW], F16)

        pm = sb("pm", [P, 2, 4, NBLK], F32)
        nmx = sb("nmx", [BLK, 2, NBLK], F32)
        nm = sb("nm", [P, 2, NBLK], BF16)
        i2 = sb("i2", [P, BLK], BF16)
        ph = sb("ph", [P, H, B, T], F16)
        pl = sb("pl", [P, H, B, T], F16)
        wfh = sb("wfh", [P, 2 * HID, P], F32R)
        wfl = sb("wfl", [P, 2 * HID, P], F32R)
        x2h = sb("x2h", [P, B * T], F32R)
        x2l = sb("x2l", [P, B * T], F32R)
        rec = sb("rec", [P, B, H], F32)
        r8 = sb("r8", [P, 12, B], F32)

        ph_f = ph[:, :, :, :].rearrange("p h b t -> p (h b t)").bitcast(F32)
        pl_f = pl[:, :, :, :].rearrange("p h b t -> p (h b t)").bitcast(F32)
        qd_f = qd[:, :, :, :, :].rearrange("p g s h t -> p (g s h t)").bitcast(F32)
        wf = ph_f[:, 0:2 * HID * P].rearrange("p (n c) -> p n c", c=P)

        place = [0]

        def late(n, parts=P):
            a = place[0]
            place[0] = a + n
            return qd_f[0:parts, a:a + n]

        def per_batch(v):
            return v.rearrange("p (b c) -> p b c", b=B)

        ctxv = late(B * H * DH).rearrange("p (b h d) -> p b h d", b=B, h=H)
        ctxT = per_batch(late(B * T))
        z = per_batch(late(B * D))
        x1 = per_batch(late(B * D))
        x1T = per_batch(late(B * T))
        p2 = per_batch(late(B * S))
        p2T = per_batch(late(B * T))
        x2 = per_batch(late(B * D))
        wd = late(HID * D).rearrange("p (n c) -> p n c", n=HID)
        cn = per_batch(late(B * D))
        ct = per_batch(late(B * S))
        sel = late(PAIRS * P // 2).bitcast(F16).rearrange("p (n c) -> p n c", n=PAIRS)
        cwT = late(B * T // 2).bitcast(F16)
        pr, key, s1, s2, cw, tie = (per_batch(late(B * E)) for _ in range(6))
        assert place[0] <= NG * HG * B * T
        th, ga, gu, hh = (ph_f[:, n * 2 * GT:(n + 1) * 2 * GT].rearrange("p (k t) -> p k t", k=2) for n in range(4))
        o_sb = per_batch(pl_f[:, 0:B * D])
        def unit(u):
            return ps[:, 2 * (u % 4):2 * (u % 4) + 2, :]

        x_in = [sem(f"x_in{g}") for g in range(G)]
        id_in, wp_in, pe_in, cl_in, rw_in, wf_in, wr_in, late_in = (
            sem(n) for n in ("id_in", "wp_in", "pe_in", "cl_in", "rw_in", "wf_in", "wr_in", "late_in"))
        kp_out, kp_in, q_out, q_in, out_done = (sem(n) for n in ("kp_out", "kp_in", "q_out", "q_in", "out_done"))
        dve_step = sem("dve_step")
        half_set, qd_zero, consts_set = sem("half_set"), sem("qd_zero"), sem("consts_set")
        var_ready, rstd_ready, xh_ready = sem("var_ready"), sem("rstd_ready"), sem("xh_ready")
        xT_ps, xnT_ready, qb_ready = sem("xT_ps"), sem("xnT_ready"), sem("qb_ready")
        p_ps, k_ps, q_ps, v_ps = sem("p_ps"), sem("k_ps"), sem("q_ps"), sem("v_ps")
        kp_hi, kp_lo, q_hi, q_lo = sem("kp_hi"), sem("kp_lo"), sem("q_hi"), sem("q_lo")
        v_sum, v_hi, v_lo = sem("v_sum"), sem("v_hi"), sem("v_lo")
        wf_hi, wf_lo, xb_ready = sem("wf_hi"), sem("wf_lo"), sem("xb_ready")
        scores, shift_ready, shifted = sem("scores"), sem("shift_ready"), sem("shifted")
        p_f32, p_hi, p_lo = sem("p_f32"), sem("p_hi"), sem("p_lo")
        pv_ps, ctxv_ready, ctxT_ps, ctxT_ready, y1_ps = (
            sem(n) for n in ("pv_ps", "ctxv_ready", "ctxT_ps", "ctxT_ready", "y1_ps"))
        x1_ready, x1T_ps, x1T_ready, s2_ps, nm2_ready, p2_ready, p2T_ps, p2T_ready, o2_ps = (
            sem(n) for n in ("x1_ready", "x1T_ps", "x1T_ready", "s2_ps", "nm2_ready", "p2_ready", "p2T_ps",
                             "p2T_ready", "o2_ps"))
        x2_ready, x2T_ps, x2T_ready, x2h_ready, x2l_ready = (
            sem(n) for n in ("x2_ready", "x2T_ps", "x2T_ready", "x2h_ready", "x2l_ready"))
        lg_ps, lg_ready, pr_ready, cw_ready, cwT_ps, cwT_hi, cwT_ready = (
            sem(n) for n in ("lg_ps", "lg_ready", "pr_ready", "cw_ready", "cwT_ps", "cwT_hi", "cwT_ready"))
        gu_ps, cwr_ps, th_ready, ga_ready, hid_ready, y_step, o_ready = (
            sem(n) for n in ("gu_ps", "cwr_ps", "th_ready", "ga_ready", "hid_ready", "y_step", "o_ready"))

        block = es.enter_context(nc.Block())

        @block.sync
        def _(sp):
            for g in range(G):
                sp.dma_start(x_sb[:, g * GB:(g + 1) * GB, :],
                             x[g * GB:(g + 1) * GB].rearrange("b t d -> t b d")).then_inc(x_in[g], 16)
            sp.dma_start(ident[:, :], ident_d).then_inc(id_in, 16)
            sp.dma_start(rw[:, :, :], rows.partition_broadcast(P)).then_inc(rw_in, 16)
            sp.dma_start(wf, w_ffn.rearrange("p (n c) -> p n c", c=P)).then_inc(wf_in, 16)
            sp.dma_start(wr[:, :], w_r).then_inc(wr_in, 16)

            def rows_of(scr, part):
                return scr[:, part].rearrange("h d g t -> h (d g) t")

            sp.wait_ge(kp_hi, 1 + G)
            for part in (0, 1):
                sp.dma_start(rows_of(kp_scr, part), kp_c[:, 0, :]).then_inc(kp_out, 16)
            sp.wait_ge(kp_lo, 1 + G)
            for part in (2, 3):
                sp.dma_start(rows_of(kp_scr, part), kp_c[:, 1, :]).then_inc(kp_out, 16)
            q_rows = q_scr.rearrange("h p d g s t -> h p d g (s t)")
            sp.wait_ge(q_hi, 2 * G)
            for part in (0, 2):
                sp.dma_start(rows_of(q_rows, part), q_c[:, 0, :, :].rearrange("p s t -> p (s t)")).then_inc(q_out, 16)
            sp.wait_ge(q_lo, 2 * G)
            for part in (1, 3):
                sp.dma_start(rows_of(q_rows, part), q_c[:, 1, :, :].rearrange("p s t -> p (s t)")).then_inc(q_out, 16)
            sp.wait_ge(kp_out, 64)
            sp.dma_start(kp[:, :, :], kp_scr.rearrange("h p d g t -> (h p d) g t")).then_inc(kp_in, 16)
            sp.wait_ge(q_out, 64)
            sp.wait_ge(qd_zero, 4)
            for h in range(HG):
                sp.dma_start(qd[32 * h:32 * h + 32, :, :, h, :].rearrange("p g s t -> p (g s) t"),
                             q_scr[h].rearrange("p d g s t -> (p d) (g s) t")).then_inc(q_in, 16)
            sp.wait_ge(scores, UNITS)
            sp.dma_start(ct, ctx_t.rearrange("p (b s) -> p b s", b=B)).then_inc(late_in, 16)
            sp.dma_start(cn[0:S], ctx_n.rearrange("b s d -> s b d")).then_inc(late_in, 16)
            sp.dma_start(tie, tie_d.partition_broadcast(P)).then_inc(late_in, 16)
            sp.dma_start(sel[0:64], sel_d).then_inc(late_in, 16)
            sp.dma_start(wd, w_down.rearrange("p (n c) -> p n c", c=D)).then_inc(late_in, 16)
            for g in range(G):
                sp.wait_ge(o_ready, g + 1)
                sp.dma_start(out[g * GB:(g + 1) * GB].rearrange("b t d -> t b d"),
                             o_sb[:, g * GB:(g + 1) * GB, :]).then_inc(out_done, 16)
            sp.wait_ge(out_done, 16 * G)

        @block.gpsimd
        def _(pool):
            nc.gpsimd.memset(half[:, :], -0.5).then_inc(half_set, 1)

            def power(n):
                g = n % G
                pool.wait_ge(var_ready, n + 1)
                nc.gpsimd.tensor_tensor(rstd[:, g * GB:(g + 1) * GB], ve[:, g * GB:(g + 1) * GB],
                                        half[:, g * GB:(g + 1) * GB], ALU.pow).then_inc(rstd_ready, 1)

            pool.wait_ge(half_set, 1)
            quarter = NG * HG * B * T // 4
            for n in range(4):
                nc.gpsimd.memset(qd_f[:, n * quarter:(n + 1) * quarter].bitcast(U32), 0).then_inc(qd_zero, 1)
                if n < G:
                    power(n)
            nc.gpsimd.memset(nm[:, :, :], 0.0).then_inc(consts_set, 1)
            nc.gpsimd.memset(i2[:, :], 0.0).then_inc(consts_set, 1)
            nc.gpsimd.memset(vp[:, :, :, VW - 1:VW], 1.0).then_inc(consts_set, 1)
            pool.wait_ge(consts_set, 3)
            pool.wait_ge(id_in, 16)
            for n in range(2):
                nc.gpsimd.tensor_copy(i2[n * BLK:(n + 1) * BLK, :], ident[0:BLK, 0:BLK]).then_inc(consts_set, 1)
                pool.wait_ge(consts_set, 4 + n)
            pool.wait_ge(xh_ready, G)
            pool.wait_ge(rw_in, 16)
            for g in range(G):
                xg = x_sb[:, g * GB:(g + 1) * GB, :]
                nc.gpsimd.tensor_tensor(xg, xg, rw[:, 1:2, :].broadcast_to([P, GB, D]), ALU.add).then_inc(xb_ready, 1)
            pool.wait_ge(wf_hi, 1)
            nc.gpsimd.tensor_tensor(wfl[:, :, :], wf, wfh[:, :, :].bitcast(F32), ALU.subtract).then_inc(wf_lo, 1)
            for u in range(UNITS):
                c, hf = u // 2, u % 2
                pool.wait_ge(p_hi, u + 1)
                rows_u = slice(8 * hf, 8 * hf + 8)
                hi = ph[:, rows_u, :, CI * c:CI * c + CI].rearrange("p h b i -> p (h b) i")
                lo = pl[:, rows_u, :, CI * c:CI * c + CI].rearrange("p h b i -> p (h b) i")
                nc.gpsimd.tensor_tensor(lo, p32[:, u % 2, :].rearrange("p (n i) -> p n i", i=CI), hi,
                                        ALU.subtract).then_inc(p_lo, 1)
            for n in range(G, 4 * G):
                power(n)

        @block.scalar
        def _(act):
            act.dma_start(cl[:, :], cols).then_inc(cl_in, 16)
            act.dma_start(pe_sb[:, :], pos_emb).then_inc(pe_in, 16)
            act.dma_start(wp[:, :, :], w_proj.rearrange("p (n c) -> p n c", n=5)).then_inc(wp_in, 16)

            def split_hi(dst, src, bias=0.0):
                return nc.scalar.activation(dst, src, ACT.Identity, bias=bias)

            act.wait_ge(p_ps, 1)
            split_hi(kp_c[:, 0, B * T:KPT], ps[:, 2, 0:POS]).then_inc(kp_hi, 1)
            act.wait_ge(cl_in, 16)
            for g in range(G):
                act.wait_ge(xT_ps, g + 1)
                nc.scalar.activation(xnT[:, g * GT:(g + 1) * GT], ps[:, g, :], ACT.Identity, bias=cl[:, 5:6],
                                     scale=cl[:, 4:5]).then_inc(xnT_ready, 1)
            for g in range(G):
                act.wait_ge(k_ps, g + 1)
                split_hi(kp_c[:, 0, g * GT:(g + 1) * GT], ps[:, 3 + g, :], cl[:, 1:2]).then_inc(kp_hi, 1)
            act.wait_ge(qb_ready, 2)
            for g in range(G):
                act.wait_ge(q_ps, g + 1)
                for s in range(2):
                    split_hi(q_c[:, 0, s, g * GT:(g + 1) * GT], ps[:, 5 + g, :], qb[:, s:s + 1]).then_inc(q_hi, 1)
            for g in range(G):
                act.wait_ge(v_sum, g + 1)
                split_hi(vp[:, g * GB:(g + 1) * GB, :, 0:DH].rearrange("p b h d -> p (b h) d"),
                         v32[:, g * GB:(g + 1) * GB, :].rearrange("p b (h d) -> p (b h) d", d=DH)).then_inc(v_hi, 1)
            act.wait_ge(wf_in, 16)
            nc.scalar.activation(wfh[:, :, :], wf, ACT.Copy).then_inc(wf_hi, 1)

            for u in range(UNITS):
                c, hf = u // 2, u % 2
                act.wait_ge(shifted, u + 1)
                if u == 0:
                    act.wait_ge(wf_lo, 1)
                    act.wait_ge(q_in, 16 * HG)
                if u >= 2:
                    act.wait_ge(p_lo, u - 1)
                nc.scalar.activation(p32[:, u % 2, :].rearrange("p (k n) -> p k n", k=2), unit(u), ACT.Exp,
                                     scale=SC).then_inc(p_f32, 1)
                nc.scalar.activation(ph[:, 8 * hf:8 * hf + 8, :, CI * c:CI * c + CI].rearrange("p h b i -> p (h b) i"),
                                     unit(u).rearrange("p k (n i) -> p (k n) i", i=CI), ACT.Exp,
                                     scale=SC).then_inc(p_hi, 1)

            def group(v, g):
                return v[:, g * GB:(g + 1) * GB]

            for g in range(G):
                act.wait_ge(ctxT_ps, g + 1)
                nc.scalar.copy(group(ctxT, g), ps[:, 4 * g, :].rearrange("p (b t) -> p b t", b=GB)).then_inc(ctxT_ready, 1)
            for g in range(G):
                act.wait_ge(x1T_ps, g + 1)
                nc.scalar.copy(group(x1T, g), ps[:, 4 * g + 2, :].rearrange("p (b t) -> p b t", b=GB)).then_inc(x1T_ready, 1)
            for g in range(G):
                act.wait_ge(nm2_ready, g + 1)
                for j in range(GB):
                    b = g * GB + j
                    nc.scalar.activation(p2[:, b, :], ps[:, 4 * g + 3, j * S:(j + 1) * S], ACT.Exp,
                                         bias=r8[:, 0, b:b + 1], accum_out=r8[:, 1, b:b + 1]).then_inc(p2_ready, 1)
            for g in range(G):
                act.wait_ge(p2T_ps, g + 1)
                nc.scalar.copy(p2T[0:S, g * GB:(g + 1) * GB],
                               ps[0:S, 4 * g, :].rearrange("p (b t) -> p b t", b=GB)).then_inc(p2T_ready, 1)
            for g in range(G):
                act.wait_ge(x2T_ps, g + 1)
                nc.scalar.activation(x2h[:, g * GT:(g + 1) * GT], ps[:, 4 * g + 2, :], ACT.Copy).then_inc(x2h_ready, 1)
                nc.scalar.copy(x2T[:, g * GT:(g + 1) * GT], ps[:, 4 * g + 2, :]).then_inc(x2T_ready, 1)

            def tanh(k):
                act.wait_ge(gu_ps, k + 1)
                if k >= 2:
                    act.wait_ge(ga_ready, k - 1)
                nc.scalar.activation(th[:, k % 2, :], ps[:, k % 2, :], ACT.Tanh, scale=0.5).then_inc(th_ready, 1)

            for g in range(G):
                act.wait_ge(lg_ready, g + 1)
                nc.scalar.activation(group(pr, g), group(pr, g), ACT.Exp).then_inc(pr_ready, 1)
            tanh(0)
            for g in range(G):
                act.wait_ge(cwT_ps, g + 1)
                nc.scalar.copy(cwT[0:E, g * GT:(g + 1) * GT], ps[0:E, 5 - g, :]).then_inc(cwT_hi, 1)
            for k in range(1, NK):
                tanh(k)

        @block.vector
        def _(dve):
            steps = [0]

            def link(ins):
                steps[0] += 1
                ins.then_inc(dve_step, 1)
                dve.wait_ge(dve_step, steps[0])

            def group(v, g):
                return v[:, g * GB:(g + 1) * GB]

            def stats(src, g):
                for b in range(g * GB, (g + 1) * GB):
                    last = nc.vector.bn_stats(st[:, b, :], src[:, b, :])
                link(last)
                for b in range(g * GB, (g + 1) * GB):
                    last = nc.vector.bn_aggr(mv[:, b, :], st[:, b, :])
                link(last)
                nc.vector.tensor_scalar_add(group(ve, g), group(mv, g)[:, :, 1], EPS).then_inc(var_ready, 1)

            def norm(n, dst, src, ready):
                g = n % G
                dve.wait_ge(rstd_ready, n + 1)
                for b in range(g * GB, (g + 1) * GB):
                    last = nc.vector.tensor_scalar(dst[:, b, :], src[:, b, :], mv[:, b, 0:1], rstd[:, b:b + 1],
                                                   ALU.subtract, ALU.mult)
                last.then_inc(ready, 1)

            for g in range(G):
                dve.wait_ge(x_in[g], 16)
                stats(x_sb, g)
            dve.wait_ge(cl_in, 16)
            for s in range(2):
                nc.vector.tensor_tensor(qb[:, s:s + 1], cl[:, 0:1], cl[:, 2 + s:3 + s], ALU.add).then_inc(qb_ready, 1)
            for g in range(G):
                norm(g, xh, x_sb, xh_ready)

            dve.wait_ge(kp_hi, 1)
            nc.vector.tensor_tensor(kp_c[:, 1, B * T:KPT], ps[:, 2, 0:POS], kp_c[:, 0, B * T:KPT],
                                    ALU.subtract).then_inc(kp_lo, 1)
            for g in range(G):
                cols_g = slice(g * GT, (g + 1) * GT)
                dve.wait_ge(kp_hi, 2 + g)
                nc.vector.scalar_tensor_tensor(out=kp_c[:, 1, cols_g], in0=ps[:, 3 + g, :], scalar=cl[:, 1:2],
                                               in1=kp_c[:, 0, cols_g], op0=ALU.add, op1=ALU.subtract).then_inc(kp_lo, 1)
            dve.wait_ge(qb_ready, 2)
            for g in range(G):
                cols_g = slice(g * GT, (g + 1) * GT)
                dve.wait_ge(q_hi, 2 * g + 2)
                for s in range(2):
                    nc.vector.scalar_tensor_tensor(out=q_c[:, 1, s, cols_g], in0=ps[:, 5 + g, :],
                                                   scalar=qb[:, s:s + 1], in1=q_c[:, 0, s, cols_g],
                                                   op0=ALU.add, op1=ALU.subtract).then_inc(q_lo, 1)
            dve.wait_ge(rw_in, 16)
            for g in range(G):
                dve.wait_ge(v_ps, g + 1)
                nc.vector.tensor_tensor(group(v32, g), ps[:, (7, 2)[g], :].rearrange("p (b c) -> p b c", b=GB),
                                        rw[:, 0:1, :].broadcast_to([P, GB, D]), ALU.add).then_inc(v_sum, 1)
            for g in range(G):
                dve.wait_ge(v_hi, g + 1)
                nc.vector.tensor_tensor(group(vp, g)[:, :, :, DH:2 * DH].rearrange("p b h d -> p (b h) d"),
                                        group(v32, g).rearrange("p b (h d) -> p (b h) d", d=DH),
                                        group(vp, g)[:, :, :, 0:DH].rearrange("p b h d -> p (b h) d"),
                                        ALU.subtract).then_inc(v_lo, 1)

            dve.wait_ge(consts_set, 5)
            for u in range(UNITS):
                m = u % 2
                dve.wait_ge(scores, u + 1)
                link(nc.vector.tensor_reduce(pm[:, m, 0, :], unit(u).rearrange("p k (n c) -> p (k n) c", c=BLK), AX,
                                             ALU.max, apply_transpose=True))
                for q in range(1, 4):
                    last = nc.vector.tensor_copy(pm[0:BLK, m, q, :], pm[BLK * q:BLK * (q + 1), m, 0, :])
                link(last)
                link(nc.vector.tensor_reduce(nmx[:, m, :], pm[0:BLK, m, :, :].rearrange("p q n -> p n q"), AX,
                                             ALU.max, negate=True))
                if u >= 2:
                    dve.wait_ge(shifted, u - 1)
                link(nc.vector.tensor_copy(nm[0:BLK, m, :], nmx[:, m, :]))
                nc.vector.tensor_tensor(nm[BLK:2 * BLK, m, :], nmx[:, m, :], nm[0:BLK, m, :],
                                        ALU.subtract).then_inc(shift_ready, 1)

            for g in range(G):
                for j in range(GB):
                    b = g * GB + j
                    dve.wait_ge(pv_ps, b + 1)
                    u_b = ps[:, b, 0:H * VW].rearrange("p (h w) -> p h w", h=H)
                    nc.vector.reciprocal(rec[:, b, :], u_b[:, :, VW - 1])
                    last = nc.vector.tensor_reduce(ctxv[:, b], u_b[:, :, 0:2 * DH].rearrange("p h (k d) -> p h d k", k=2),
                                                   AX, ALU.add)
                link(last)
                nc.vector.tensor_tensor(group(ctxv, g).rearrange("p b h d -> p (b h) d"),
                                        group(ctxv, g).rearrange("p b h d -> p (b h) d"),
                                        group(rec, g).rearrange("p b (h o) -> p (b h) o", o=1).broadcast_to([P, GB * H, DH]),
                                        ALU.mult).then_inc(ctxv_ready, 1)
            dve.wait_ge(xb_ready, G)
            for g in range(G):
                dve.wait_ge(y1_ps, g + 1)
                link(nc.vector.tensor_tensor(group(z, g), ps[:, 4 * g + 1, :].rearrange("p (b c) -> p b c", b=GB),
                                             group(x_sb, g), ALU.add))
                stats(z, g)
            for g in range(G):
                norm(G + g, x1, z, x1_ready)
            for g in range(G):
                dve.wait_ge(s2_ps, g + 1)
                nc.vector.tensor_reduce(r8[:, 0, g * GB:(g + 1) * GB],
                                        ps[:, 4 * g + 3, 0:GB * S].rearrange("p (b s) -> p b s", b=GB), AX, ALU.max,
                                        negate=True).then_inc(nm2_ready, 1)
            for g in range(G):
                dve.wait_ge(o2_ps, g + 1)
                link(nc.vector.reciprocal(r8[:, 2, g * GB:(g + 1) * GB], r8[:, 1, g * GB:(g + 1) * GB]))
                for j in range(GB):
                    b = g * GB + j
                    last = nc.vector.scalar_tensor_tensor(out=z[:, b, :], in0=ps[:, 4 * g + 1, j * D:(j + 1) * D],
                                                          scalar=r8[:, 2, b:b + 1], in1=x1[:, b, :],
                                                          op0=ALU.mult, op1=ALU.add)
                link(last)
                stats(z, g)
            for g in range(G):
                norm(2 * G + g, x2, z, x2_ready)
            for g in range(G):
                cols_g = slice(g * GT, (g + 1) * GT)
                dve.wait_ge(x2h_ready, g + 1)
                dve.wait_ge(x2T_ready, g + 1)
                nc.vector.tensor_tensor(x2l[:, cols_g], x2T[:, cols_g], x2h[:, cols_g].bitcast(F32),
                                        ALU.subtract).then_inc(x2l_ready, 1)

            def spread(v, g):
                return r8[:, v, g * GB:(g + 1) * GB].rearrange("p (b o) -> p b o", o=1).broadcast_to([P, GB, E])

            def scalar_of(v, g):
                return r8[:, v, g * GB:(g + 1) * GB]

            for g in range(G):
                logits = ps[:, 4 * g + 3, 0:GB * E].rearrange("p (b e) -> p b e", b=GB)
                dve.wait_ge(lg_ps, g + 1)
                link(nc.vector.tensor_reduce(scalar_of(3, g), logits, AX, ALU.max))
                nc.vector.tensor_tensor(group(pr, g), logits, spread(3, g), ALU.subtract).then_inc(lg_ready, 1)
            dve.wait_ge(late_in, 80)
            for g in range(G):
                dve.wait_ge(pr_ready, g + 1)
                p_g, key_g, s1_g, s2_g, tie_g, cw_g = (group(v, g) for v in (pr, key, s1, s2, tie, cw))
                nc.vector.tensor_reduce(scalar_of(4, g), p_g, AX, ALU.add)
                link(nc.vector.tensor_reduce(scalar_of(5, g), p_g, AX, ALU.max))
                nc.vector.reciprocal(scalar_of(6, g), scalar_of(4, g))
                link(nc.vector.tensor_tensor(key_g, p_g, spread(5, g), ALU.is_equal))
                link(nc.vector.tensor_tensor(key_g, key_g, tie_g, ALU.mult))
                link(nc.vector.tensor_reduce(scalar_of(7, g), key_g, AX, ALU.max))
                link(nc.vector.tensor_tensor(s1_g, key_g, spread(7, g), ALU.is_equal))
                link(nc.vector.scalar_tensor_tensor(out=s2_g, in0=s1_g, scalar=-BIG, in1=p_g, op0=ALU.mult, op1=ALU.add))
                link(nc.vector.tensor_reduce(scalar_of(8, g), s2_g, AX, ALU.max))
                link(nc.vector.tensor_tensor(key_g, s2_g, spread(8, g), ALU.is_equal))
                link(nc.vector.tensor_tensor(key_g, key_g, tie_g, ALU.mult))
                link(nc.vector.tensor_reduce(scalar_of(9, g), key_g, AX, ALU.max))
                link(nc.vector.tensor_tensor(s2_g, key_g, spread(9, g), ALU.is_equal))
                link(nc.vector.tensor_tensor(s1_g, s1_g, s2_g, ALU.add))
                link(nc.vector.tensor_tensor(s1_g, s1_g, p_g, ALU.mult))
                nc.vector.tensor_tensor(cw_g, s1_g, spread(6, g), ALU.mult).then_inc(cw_ready, 1)

            def hidden(k):
                m = k % 2
                dve.wait_ge(th_ready, k + 1)
                if k >= 2:
                    dve.wait_ge(y_step, k - 1)
                nc.vector.scalar_tensor_tensor(out=ga[:, m, :], in0=th[:, m, :], scalar=1.0, in1=ps[:, m, :],
                                               op0=ALU.add, op1=ALU.mult).then_inc(ga_ready, 1)
                dve.wait_ge(ga_ready, k + 1)
                link(nc.vector.tensor_tensor(gu[:, m, :], ga[:, m, :], ps[:, 2 + m, :], ALU.mult))
                if k % HID == 0:
                    nc.vector.tensor_scalar(hh[:, m, :], gu[:, m, :], 0.5, None, ALU.mult).then_inc(hid_ready, 1)
                else:
                    dve.wait_ge(cwr_ps, k - k // HID)
                    nc.vector.tensor_tensor(hh[:, m, :], gu[:, m, :], ps[:, 4 + m, :], ALU.mult).then_inc(hid_ready, 1)

            hidden(0)
            for g in range(G):
                dve.wait_ge(cwT_hi, g + 1)
                nc.vector.tensor_tensor(cwT[32:32 + E, g * GT:(g + 1) * GT], ps[0:E, 5 - g, :],
                                        cwT[0:E, g * GT:(g + 1) * GT], ALU.subtract).then_inc(cwT_ready, 1)

            def final(g):
                dve.wait_ge(y_step, HID * (g + 1))
                link(nc.vector.tensor_tensor(group(z, g), ps[:, 6 + g, :].rearrange("p (b c) -> p b c", b=GB),
                                             group(x2, g), ALU.add))
                stats(z, g)

            for k in range(1, NK):
                hidden(k)
                if k == HID + 1:
                    final(0)
                if k == HID + 3:
                    norm(3 * G, o_sb, z, o_ready)
            final(1)
            norm(3 * G + 1, o_sb, z, o_ready)

        @block.tensor
        def _(pe):
            def mm(o, w, r, start, stop):
                return nc.tensor.matmul(o, w, r, start=start, stop=stop, skip_group_check=True)

            def transposes(bank, src, ready, done, rows_out=P):
                for g in range(G):
                    pe.wait_ge(ready, ready_at(g))
                    for j in range(GB):
                        last = nc.tensor.transpose(ps[0:rows_out, bank(g), j * T:(j + 1) * T], src(g * GB + j), ident[:, :])
                    last.then_inc(done, 1)

            ready_at = lambda g: g + 1
            pe.wait_ge(pe_in, 16)
            pe.wait_ge(wp_in, 16)
            mm(ps[:, 2, 0:POS], wp[:, 2, :], pe_sb[:, :], True, True).then_inc(p_ps, 1)
            pe.wait_ge(id_in, 16)
            transposes(lambda g: g, lambda b: xh[:, b, :], xh_ready, xT_ps)
            for g in range(G):
                pe.wait_ge(xnT_ready, g + 1)
                mm(ps[:, 3 + g, :], wp[:, 1, :], xnT[:, g * GT:(g + 1) * GT], True, True).then_inc(k_ps, 1)
                mm(ps[:, 5 + g, :], wp[:, 0, :], xnT[:, g * GT:(g + 1) * GT], True, True).then_inc(q_ps, 1)
            pe.wait_ge(kp_lo, 1)
            for g in range(G):
                for j in range(GB):
                    b = g * GB + j
                    last = mm(ps[:, (7, 2)[g], j * D:(j + 1) * D], xnT[:, b * T:(b + 1) * T], wp[:, 3, :], j == 0, True)
                last.then_inc(v_ps, 1)

            def unit_scores(u):
                c, hf = u // 2, u % 2
                i0 = CI * c
                for k in range(2):
                    g = 2 * hf + k
                    bank = ps[:, 2 * (u % 4) + k, :].rearrange("p (h b i) -> p h b i", h=HG, b=B)
                    for b in range(B):
                        mm(bank[:, :, b, :], kp[:, g, b * T:(b + 1) * T], qd[:, g, 0, :, b * T + i0:b * T + i0 + CI],
                           b == 0, False)
                    for i in range(i0, i0 + CI):
                        a = B * T + T - 1 - i
                        last = mm(bank[:, :, :, i - i0], kp[:, g, a:a + T], qd[:, g, 1, :, i:B * T:T], False, False)
                last.then_inc(scores, 1)

            def unit_shift(u):
                pe.wait_ge(shift_ready, u + 1)
                for n in range(NBLK):
                    last = mm(unit(u)[:, n // 16, (n % 16) * BLK:(n % 16 + 1) * BLK],
                              nm[:, u % 2, n:n + 1].to_broadcast([P, P]), i2[:, :], False, True)
                last.then_inc(shifted, 1)

            pe.wait_ge(kp_in, 16)
            pe.wait_ge(q_in, 16 * HG)
            pe.wait_ge(consts_set, 5)
            for u in range(UNITS):
                if u == 1:
                    pe.wait_ge(v_sum, G)
                if u >= 4:
                    pe.wait_ge(p_hi, u - 3)
                unit_scores(u)
                if u >= 1:
                    unit_shift(u - 1)
            unit_shift(UNITS - 1)

            pe.wait_ge(v_lo, G)
            pe.wait_ge(p_lo, UNITS)
            for b in range(B):
                for h in range(H):
                    n = (h % NG) * HG + h // NG
                    o = ps[:, b, h * VW:(h + 1) * VW]
                    mm(o, ph[:, n, b, :], vp[:, b, h, :], h == 0, False)
                    last = mm(o, pl[:, n, b, :], vp[:, b, h, :], False, True)
                last.then_inc(pv_ps, 1)
            transposes(lambda g: 4 * g, lambda b: ctxv[:, b].rearrange("p h d -> p (h d)"), ctxv_ready, ctxT_ps)
            for g in range(G):
                pe.wait_ge(ctxT_ready, g + 1)
                for j in range(GB):
                    last = mm(ps[:, 4 * g + 1, j * D:(j + 1) * D], ctxT[:, g * GB + j, :], wp[:, 4, :], j == 0, True)
                last.then_inc(y1_ps, 1)
            transposes(lambda g: 4 * g + 2, lambda b: x1[:, b, :], x1_ready, x1T_ps)
            pe.wait_ge(late_in, 80)
            for g in range(G):
                pe.wait_ge(x1T_ready, g + 1)
                for j in range(GB):
                    b = g * GB + j
                    last = mm(ps[:, 4 * g + 3, j * S:(j + 1) * S], x1T[:, b, :], ct[:, b, :], j == 0, True)
                last.then_inc(s2_ps, 1)
            ready_at = lambda g: GB * (g + 1)
            transposes(lambda g: 4 * g, lambda b: p2[:, b, :], p2_ready, p2T_ps, rows_out=S)
            ready_at = lambda g: g + 1
            for g in range(G):
                pe.wait_ge(p2T_ready, g + 1)
                for j in range(GB):
                    b = g * GB + j
                    last = mm(ps[:, 4 * g + 1, j * D:(j + 1) * D], p2T[0:S, b, :], cn[0:S, b, :], j == 0, True)
                last.then_inc(o2_ps, 1)
            transposes(lambda g: 4 * g + 2, lambda b: x2[:, b, :], x2_ready, x2T_ps)
            pe.wait_ge(wr_in, 16)
            for g in range(G):
                pe.wait_ge(x2T_ready, g + 1)
                for j in range(GB):
                    b = g * GB + j
                    last = mm(ps[:, 4 * g + 3, j * E:(j + 1) * E], x2T[:, b * T:(b + 1) * T], wr[:, :], j == 0, True)
                last.then_inc(lg_ps, 1)

            def tile_of(k):
                return SHARED if k % HID == 0 else k % HID - 1

            def up(k):
                n, g = tile_of(k), k // HID
                toks = slice(g * GT, (g + 1) * GT)
                if k >= 2:
                    pe.wait_ge(hid_ready, k - 1)
                for half_, bank in ((0, k % 2), (1, 2 + k % 2)):
                    w = 2 * n + half_
                    mm(ps[:, bank, :], wfh[:, w, :], x2l[:, toks], True, False)
                    mm(ps[:, bank, :], wfl[:, w, :], x2h[:, toks], False, False)
                    last = mm(ps[:, bank, :], wfh[:, w, :], x2h[:, toks], False, True)
                last.then_inc(gu_ps, 1)
                if n != SHARED:
                    mm(ps[:, 4 + k % 2, :], sel[0:64, n, :], cwT[0:64, toks], True, True).then_inc(cwr_ps, 1)

            def down(k):
                n, g = tile_of(k), k // HID
                pe.wait_ge(hid_ready, k + 1)
                for j in range(GB):
                    last = mm(ps[:, 6 + g, j * D:(j + 1) * D], hh[:, k % 2, j * T:(j + 1) * T], wd[:, n, :],
                              k % HID == 0 and j == 0, k % HID == HID - 1)
                last.then_inc(y_step, 1)

            pe.wait_ge(wf_lo, 1)
            pe.wait_ge(x2l_ready, 1)
            up(0)
            pe.wait_ge(x2l_ready, G)
            for g in range(G):
                pe.wait_ge(cw_ready, g + 1)
                for j in range(GB):
                    last = nc.tensor.transpose(ps[0:E, 5 - g, j * T:(j + 1) * T], cw[:, g * GB + j, :], ident[:, :])
                last.then_inc(cwT_ps, 1)
            pe.wait_ge(cwT_ready, G)
            for k in range(1, NK):
                up(k)
                down(k - 1)
            down(NK - 1)


def kernel(**inputs):
    import math
    import numpy as np
    import concourse.bacc as bacc
    from concourse.bass_utils import run_bass_kernel_spmd

    def a(name):
        return np.asarray(inputs[name])

    def grouped(w):
        return w.reshape((HG, NG, DH) + w.shape[1:]).swapaxes(1, 2).reshape(w.shape)

    L = "L0_attn_"
    w_proj = np.concatenate([grouped(a(L + "Wq")).T, grouped(a(L + "Wk")).T, grouped(a(L + "Wpos")).T,
                             a(L + "Wv").T, a(L + "Wout").T], axis=1)
    cols = np.stack([grouped(a(L + "bq")), grouped(a(L + "bk")), grouped(a(L + "u_bias").reshape(D)),
                     grouped(a(L + "v_bias").reshape(D)), a(L + "ln_gamma"), a(L + "ln_beta")], axis=1)
    rows = np.stack([a(L + "bv"), a(L + "bout")])[None]
    wg = a("L0_ffn_Wg").transpose(1, 0, 2).reshape(D, PAIRS, 2 * F)
    wu = a("L0_ffn_Wu").transpose(1, 0, 2).reshape(D, PAIRS, 2 * F)
    gate = np.concatenate([wg, a("L0_ffn_Sg")[:, None]], axis=1)
    upw = np.concatenate([wu, a("L0_ffn_Su")[:, None]], axis=1)
    w_ffn = np.stack([gate, upw], axis=2).reshape(D, 2 * HID * P)
    wdn = np.concatenate([a("L0_ffn_Wd").reshape(PAIRS, 2 * F, D), a("L0_ffn_Sd")[None]], axis=0)
    w_down = wdn.transpose(1, 0, 2).reshape(P, HID * D)
    ctx = a("ctx_1024")

    dist = (T - 1 - np.arange(2 * T - 1)).astype(np.float32)
    div = np.exp(np.arange(0, D, 2, dtype=np.float32) * np.float32(-math.log(10000.0) / D))
    ang = np.abs(dist)[:, None] * div * np.sign(dist)[:, None]
    pos = np.zeros((D, POS), np.float32)
    pos[0::2, :2 * T - 1] = np.sin(ang).T
    pos[1::2, :2 * T - 1] = np.cos(ang).T
    sel = np.zeros((64, PAIRS, P), np.float16)
    for e in range(E):
        for base in (0, 32):
            sel[base + e, e // 2, (e % 2) * F:(e % 2 + 1) * F] = 0.5
    tie = np.tile((E - np.arange(E)).astype(np.float32), (1, B, 1))

    data = {
        "x": a("x"), "ctx_n": ctx, "ctx_t": ctx.transpose(2, 0, 1).reshape(D, B * S), "w_proj": w_proj,
        "w_r": a("L0_ffn_Wr"), "w_ffn": w_ffn, "w_down": w_down, "cols": cols, "rows": rows, "pos_emb": pos,
        "ident_d": np.eye(P, dtype=np.float32), "sel_d": sel, "tie_d": tie,
    }
    nc = bacc.Bacc("TRN2", target_bir_lowering=False, num_devices=1)
    arrays, args = {}, []
    for name, value in data.items():
        value = np.ascontiguousarray(value)
        arrays[f"in_{name}"] = value
        args.append(nc.dram_tensor(f"in_{name}", value.shape, mybir.dt.from_np(value.dtype), kind="ExternalInput").ap())
    out = nc.dram_tensor("out_0", (B, T, D), F32, kind="ExternalOutput").ap()
    decoder_block(nc, *args, out)
    r = run_bass_kernel_spmd(nc, [arrays], core_ids=[0])
    return r.results[0]["out_0"]
```

```python
from contextlib import ExitStack

import concourse.bass as bass
from concourse import mybir

P = 128
ALU = mybir.AluOpType
ACT = mybir.ActivationFunctionType
AX = mybir.AxisListType.X
F32 = mybir.dt.float32
F32R = mybir.dt.float32r
F16 = mybir.dt.float16
BF16 = mybir.dt.bfloat16
U32 = mybir.dt.uint32

B, T, D = 8, 128, 128
S = 77
H, DH = 16, 8
E, F = 16, 64
HG = 4
NG = H // HG
PARTS = 4
POS = 2 * T
KPT = B * T + POS
CI = 16
NCH = T // CI
GL = 2
HF = NG // GL
UNITS = NCH * HF
SLOTS = 3
IH = 2
TI = T // IH
TM = B * T // P // IH
UH = UNITS // IH
UCOL = 2 * 512
BLK = 32
NBLK = UCOL // BLK
G = 2
GN = B // G
GT = GN * T
Q = 4
QN = B // Q
PAIRS = E // 2
HID = PAIRS + 1
EPS = 1e-5
VW = 2 * DH + 1
HW = 64
SC = DH ** -0.5
BIG = 1e30
SHARED = PAIRS
NK = G * HID



def decoder_block(nc, x, ctx_n, ctx_t, w_proj, w_r, w_ffn, w_down, cols, rows, pos_emb, ident_d, sel_d, tie_d, out):
    es = ExitStack()
    with es:
        def sb(name, shape, dt):
            return es.enter_context(nc.sbuf_tensor(name, shape, dt))

        def sem(name):
            return es.enter_context(nc.semaphore(name))

        ps = es.enter_context(nc.psum_tensor("ps", [P, 8, 512], F32))
        kp_scr = nc.dram_tensor("kp_scr", (HG, PARTS, DH, NG, KPT), F16, kind="Internal").ap()
        q_scr = nc.dram_tensor("q_scr", (IH, HG, 2, DH, NG, 2, B * TI), F16, kind="Internal").ap()

        x_sb = sb("x_sb", [P, B, D], F32)
        wp = sb("wp", [P, 5, D], F32)
        wr = sb("wr", [P, E], F32)
        cl = sb("cl", [P, 6], F32)
        rw = sb("rw", [P, 2, D], F32)
        pe_sb = sb("pe_sb", [P, POS], F32)
        i_warm = sb("i_warm", [P, 512], BF16)
        ident = sb("ident", [P, P], F32)

        st = sb("st", [P, B, 6], F32)
        mv = sb("mv", [P, B, 2], F32)
        ve = sb("ve", [P, B], F32)
        half = sb("half", [P, B], F32)
        rstd = sb("rstd", [P, B], F32)
        xh = sb("xh", [P, B, D], F32)
        v32 = xh
        xnT = sb("xnT", [P, B * T], F32)
        x2T = xnT
        xnT_i = xnT[:, :].rearrange("p (b a i) -> p b a i", b=B, a=IH)
        qb = sb("qb", [P, 2], F32)
        kp_c = sb("kp_c", [P, 2, KPT], F16)
        q_c = sb("q_c", [P, 2, IH, 2, B * TI], F16)
        p32 = q_c[:, :, :, :, :].rearrange("p a i s t -> p a (i s t)").bitcast(F32)
        kp = sb("kp", [P, NG, KPT], F16)
        qd = sb("qd", [P, IH, HG, NG, 2, B, TI], F16)
        vp = sb("vp", [P, B, H, VW], F16)

        pm = sb("pm", [P, 2, 4, NBLK], F32)
        nmx = sb("nmx", [BLK, 2, NBLK], F32)
        nm = sb("nm", [P, 2, NBLK], BF16)
        i2 = sb("i2", [P, BLK], BF16)
        ph = sb("ph", [P, IH, H, B, TI], F16)
        pl = sb("pl", [P, IH, H, B, TI], F16)
        wfh = sb("wfh", [P, 2 * HID, P], F32R)
        wfl = sb("wfl", [P, 2 * HID, P], F32R)
        x2h = sb("x2h", [P, B * T], F32R)
        x2l = sb("x2l", [P, B * T], F32R)
        rec = sb("rec", [P, B, H], F32)
        r8 = sb("r8", [P, 12, B], F32)

        ph_f = ph[:, :, :, :, :].rearrange("p a h b t -> p (a h b t)").bitcast(F32)
        pl_f = pl[:, :, :, :, :].rearrange("p a h b t -> p (a h b t)").bitcast(F32)
        qd_f = qd[:, :, :, :, :, :, :].rearrange("p a h g s b t -> p (a h g s b t)").bitcast(F32)
        wf = ph_f[:, 0:2 * HID * P].rearrange("p (n c) -> p n c", c=P)

        Q_HALF = HG * NG * B * TI
        place = [0]

        def late(n, parts=P):
            a = place[0]
            place[0] = a + n
            return qd_f[0:parts, a:a + n]

        def per_tile(v):
            return v.rearrange("p (b c) -> p b c", b=B)

        ctxv = late(B * H * DH).rearrange("p (b h d) -> p b h d", b=B, h=H)
        ctxT = per_tile(late(B * T))
        x1T = ctxT
        z = per_tile(late(B * D))
        x1 = per_tile(late(B * D))
        p2 = per_tile(late(B * S))
        p2T = per_tile(late(B * T))
        cn = per_tile(late(B * D))
        ct = per_tile(late(B * S))
        pr, key, s1, s2, cw, tie = (per_tile(late(B * E)) for _ in range(6))
        assert place[0] <= Q_HALF
        place[0] = Q_HALF
        x2 = per_tile(late(B * D))
        wd = late(HID * D).rearrange("p (n c) -> p n c", n=HID)
        sel = late(PAIRS * P // 2).bitcast(F16).rearrange("p (n c) -> p n c", n=PAIRS)
        cwT = late(B * T // 2).bitcast(F16)
        assert place[0] <= IH * Q_HALF
        th, ga, gu, cwr, hh = (ph_f[:, n * 3 * GT:(n + 1) * 3 * GT].rearrange("p (k t) -> p k t", k=3) for n in range(5))
        o_sb = per_tile(pl_f[:, 0:B * D])
        def unit(u):
            return ps[:, 2 * (u % SLOTS):2 * (u % SLOTS) + 2, :]

        def place_of(u):
            return 2 * (u // 4) + u % 2, u // 2 % 2

        def batch_of(t, bl):
            return 2 * (t % TM) + bl

        def rows_of(bl):
            return slice(TI * bl, TI * (bl + 1))

        def pv_bank(t):
            return 6 if t < TM else 2 * (t % 2)

        def sems(*names):
            return [sem(n) for n in names]

        x_in = sems("x_in0", "x_in1")
        id_in, wp_in, pe_in, cl_in, rw_in, wf_in, wr_in = sems(
            "id_in", "wp_in", "pe_in", "cl_in", "rw_in", "wf_in", "wr_in")
        ctx_in, moe_in, out_done = sems("ctx_in", "moe_in", "out_done")
        kp_in, q_out = (sems(f"{n}0", f"{n}1") for n in ("kp_in", "q_out"))
        q_in = sems("q_in0", "q_in1", "q_in2")
        kp_out = sem("kp_out")
        dve_step, half_set, qd_zero, warm_set, consts_set = sems("dve_step", "half_set", "qd_zero", "warm_set", "consts_set")
        act_warm = sem("act_warm")
        var_ready, rstd_ready, xh_ready, xT_ps, xnT_ready, qb_ready = sems(
            "var_ready", "rstd_ready", "xh_ready", "xT_ps", "xnT_ready", "qb_ready")
        p_ps, k_ps, q_ps, v_ps, kp_hi, kp_lo, q_hi, q_lo = sems(
            "p_ps", "k_ps", "q_ps", "v_ps", "kp_hi", "kp_lo", "q_hi", "q_lo")
        v_sum, v_hi, v_lo, wf_hi, wf_lo, xb_ready = sems("v_sum", "v_hi", "v_lo", "wf_hi", "wf_lo", "xb_ready")
        scores, shift_ready, shifted, p_f32, p_hi, p_lo = sems(
            "scores", "shift_ready", "shifted", "p_f32", "p_hi", "p_lo")
        pv_ps, ctxv_ready, ctxT_ps, ctxT_ready, y1_ps = sems("pv_ps", "ctxv_ready", "ctxT_ps", "ctxT_ready", "y1_ps")
        x1_ready, x1T_ps, x1T_ready, s2_ps, nm2_ready, p2_ready, p2T_ps, p2T_ready, o2_ps = sems(
            "x1_ready", "x1T_ps", "x1T_ready", "s2_ps", "nm2_ready", "p2_ready", "p2T_ps", "p2T_ready", "o2_ps")
        z_ready, ctxu_ready = sems("z_ready", "ctxu_ready")
        x2_ready, x2T_ps, x2h_ready, x2T_ready, x2l_ready = sems(
            "x2_ready", "x2T_ps", "x2h_ready", "x2T_ready", "x2l_ready")
        lg_ps, lg_ready, pr_ready, cw_ready, cwT_ps, cwT_hi, cwT_ready = sems(
            "lg_ps", "lg_ready", "pr_ready", "cw_ready", "cwT_ps", "cwT_hi", "cwT_ready")
        gate_ps, up_ps, th_ready, ga_ready, gu_ready, cwr_ps, cwr_ready, hid_ready, y_tile, o_ready = sems(
            "gate_ps", "up_ps", "th_ready", "ga_ready", "gu_ready", "cwr_ps", "cwr_ready", "hid_ready", "y_tile",
            "o_ready")

        def steps(text):
            return [(w.rstrip("0123456789"), int(w[len(w.rstrip("0123456789")):])) for w in text.split()]

        PE_STEPS = steps("""
            scores0 scores1 shift0 scores2 shift1 scores3 shift2 scores4 shift3 scores5 shift4 scores6
            shift5 scores7 shift6 scores8 shift7 scores9 shift8 scores10 shift9 pv0 scores11 shift10 pv1
            scores12 shift11 ctxT0 scores13 shift12 pv2 scores14 shift13 scores15 shift14 pv3 shift15 attn0
            warm1 warm6 ctxT1 warm1 attn1 norm0 warm1 cross0 warm1 pv4 probs0 pv5 norm1 pv6 mix0 cross1
            warm2 pv7 ctxT2 probs1 warm2 mix1 attn2 warm3 ctxT3 warm2 attn3 warm2 next0 warm6 next1 lg0 lg1
            gate_up0 norm2 norm3 cross2 cross3 gate_up1 gate_up2 probs2 down0 mix2 cwT0 gate_up3 probs3 cwr1
            gate_up4 cwr2 gate_up5 mix3 cwr3 down1 cwr4 down2 cwr5 down3 gate_up6 next2 cwr6 gate_up7 next3
            cwr7 gate_up8 lg2 lg3 down4 cwr8 gate_up9 down5 gate_up10 down6 cwT1 down7 gate_up11 cwr10 down8
            gate_up12 cwr11 gate_up13 down9 cwr12 down10 gate_up14 cwr13 down11 cwr14 gate_up15 down12
            gate_up16 cwr15 gate_up17 cwr16 down13 cwr17 down14 down15 down16 down17""")
        ACT_STEPS = steps("""
            shift0 shift1 shift2 shift3 shift4 shift5 shift6 shift7 shift8 shift9 shift10 shift11 ctxT0
            shift12 shift13 shift14 shift15 ctxT1 norm0 cross0 probs0 norm1 cross1 ctxT2 probs1 ctxT3 next0
            next1 gate_up0 norm2 router0 norm3 cross2 gate_up1 gate_up2 probs2 cross3 cwT0 gate_up3 cwr1
            probs3 gate_up4 cwr2 cwr3 cwr4 gate_up5 cwr5 gate_up6 cwr6 next2 gate_up7 cwr7 gate_up8 next3
            router1 gate_up9 cwr8 gate_up10 cwT1 gate_up11 cwr10 gate_up12 gate_up13 cwr11 cwr12 gate_up14
            cwr13 gate_up15 cwr14 gate_up16 cwr15 gate_up17 cwr16 cwr17""")
        DVE_STEPS = steps("""
            scores0 scores1 scores2 scores3 scores4 scores5 scores6 scores7 scores8 scores9 scores10 pv0
            scores11 pv1 scores12 scores13 pv2 scores14 scores15 pv3 attn0 norm0 attn1 cross0 norm1 pv4 pv5
            pv6 cross1 mix0 pv7 mix1 next0 attn2 next1 attn3 router0 norm2 norm3 hidden0 cross2 cross3 pick0
            hidden1 cwT0 hidden2 hidden3 mix2 mix3 hidden4 next2 hidden5 next3 hidden6 hidden7 hidden8
            router1 pick1 hidden9 cwT1 hidden10 hidden11 y0 hidden12 hidden13 y1 o0 hidden14 o1 hidden15
            hidden16 hidden17 y2 y3 o2 o3""")
        POOL_STEPS = steps("""
            shift0 shift1 shift2 shift3 shift4 shift5 shift6 shift7 shift8 shift9 pv0 pv1 shift10 shift11
            shift12 pv2 shift13 pv3 shift14 attn0 shift15 attn1 pv4 pv5 mix0 pv6 pv7 mix1 rest0 attn2 rest1
            attn3 hidden1 hidden2 hidden3 mix2 hidden4 mix3 hidden5 rest2 hidden6 rest3 hidden7 hidden8
            hidden10 y0 hidden11 hidden12 y1 hidden13 hidden14 hidden15 hidden16 hidden17 y2 y3""")

        NORMS = [s for s in DVE_STEPS if s[0] in ("attn", "mix", "y")]

        def norm_no(stage, q):
            return Q + NORMS.index((stage, q))

        def mid(q):
            return 6 + q % 2

        def y_place(b):
            return (5, b * D) if b < GN else (6 + (b - GN) // QN, (b - GN) % QN * D)

        CW_BANK = 4
        WARM_BANK = 5

        def routed(k):
            return k % HID != 0

        def n_routed(k):
            return k - k // HID

        def read_q(queue, ih, groups, done):
            queue.wait_ge(q_out[ih], 32)
            queue.wait_ge(qd_zero, 2 * (ih + 1))
            for h in range(HG):
                src = q_scr[ih, h:h + 1, :, :, groups].rearrange("o l d g s t -> o (l d) (g s t)").broadcast_to(
                    [2, 2 * DH, (groups.stop - groups.start) * 2 * B * TI])
                queue.dma_start(qd[32 * h:32 * h + 32, ih, h, groups].rearrange("p g s b t -> p (g s b t)"),
                             src).then_inc(done, 16)

        block = es.enter_context(nc.Block())

        @block.sync
        def _(sp):
            for g in range(G):
                sp.dma_start(x_sb[:, g * GN:(g + 1) * GN, :], x[:, g * GN:(g + 1) * GN, :]).then_inc(x_in[g], 16)
            sp.dma_start(ident[:, :], ident_d).then_inc(id_in, 16)
            sp.dma_start(rw[:, :, :], rows.partition_broadcast(P)).then_inc(rw_in, 16)
            sp.wait_ge(wp_in, 16)
            sp.dma_start(wf, w_ffn.rearrange("p (n c) -> p n c", c=P)).then_inc(wf_in, 16)
            sp.dma_start(wr[:, :], w_r).then_inc(wr_in, 16)

            def write_kp(part, toks):
                for place in (2 * part, 2 * part + 1):
                    sp.dma_start(kp_scr[:, place, :, :, toks].rearrange("h d g t -> h (d g) t"),
                                 kp_c[:, part, toks]).then_inc(kp_out, 16)

            def write_q(ih, part):
                sp.dma_start(q_scr[ih, :, part].rearrange("h d g s t -> h (d g) (s t)"),
                             q_c[:, part, ih, :, :].rearrange("p s t -> p (s t)")).then_inc(q_out[ih], 16)

            def read_kp(hf):
                sp.wait_ge(kp_out, 128)
                sp.dma_start(kp[:, hf * GL:(hf + 1) * GL, :],
                             kp_scr[:, :, :, hf * GL:(hf + 1) * GL].rearrange("h p d g t -> (h p d) g t")
                             ).then_inc(kp_in[hf], 16)

            table, tokens = slice(B * T, KPT), slice(0, B * T)
            for part, done in ((0, kp_hi), (1, kp_lo)):
                sp.wait_ge(done, 1)
                write_kp(part, table)
            sp.wait_ge(q_hi, 2)
            write_q(0, 0)
            sp.wait_ge(q_lo, 2)
            write_q(0, 1)
            sp.wait_ge(kp_hi, 1 + G)
            write_kp(0, tokens)
            sp.wait_ge(kp_lo, 1 + G)
            write_kp(1, tokens)
            read_kp(0)
            read_kp(1)
            read_q(sp, 0, slice(GL, NG), q_in[1])
            for part, done in ((0, q_hi), (1, q_lo)):
                sp.wait_ge(done, 2 * IH)
                write_q(1, part)
            read_q(sp, 1, slice(0, NG), q_in[2])
            sp.wait_ge(scores, UH)
            sp.dma_start(ct, ctx_t.rearrange("p (b s) -> p b s", b=B)).then_inc(ctx_in, 16)
            sp.dma_start(cn[0:S], ctx_n.rearrange("b s d -> s b d")).then_inc(ctx_in, 16)
            sp.dma_start(tie, tie_d.partition_broadcast(P)).then_inc(moe_in, 16)
            sp.wait_ge(scores, UNITS)
            sp.dma_start(sel[0:64], sel_d).then_inc(moe_in, 16)
            sp.dma_start(wd, w_down.rearrange("p (n c) -> p n c", c=D)).then_inc(moe_in, 16)
            for q in range(Q):
                sp.wait_ge(o_ready, q + 1)
                sp.dma_start(out[:, q * QN:(q + 1) * QN, :],
                             o_sb[:, q * QN:(q + 1) * QN, :]).then_inc(out_done, 16)
            sp.wait_ge(out_done, 16 * Q)

        @block.gpsimd
        def _(pool):
            nc.gpsimd.memset(half[:, :], -0.5).then_inc(half_set, 1)
            pool.wait_ge(half_set, 1)

            def power(n, q):
                pool.wait_ge(var_ready, n + 1)
                nc.gpsimd.tensor_tensor(rstd[:, q * QN:(q + 1) * QN], ve[:, q * QN:(q + 1) * QN],
                                        half[:, q * QN:(q + 1) * QN], ALU.pow).then_inc(rstd_ready, 1)

            def zero(n):
                w = 2 * HG * B * T // 2
                nc.gpsimd.memset(qd_f[:, n * w:(n + 1) * w].bitcast(U32), 0).then_inc(qd_zero, 1)

            zero(0)
            for q in range(Q):
                power(q, q)
            zero(1)
            pool.wait_ge(act_warm, 1)
            nc.gpsimd.memset(nm[:, :, :], 0.0).then_inc(consts_set, 1)
            nc.gpsimd.memset(i2[:, :], 0.0).then_inc(consts_set, 1)
            nc.gpsimd.memset(vp[:, :, :, VW - 1:VW], 1.0).then_inc(consts_set, 1)
            pool.wait_ge(consts_set, 3)
            pool.wait_ge(id_in, 16)
            for n in range(2):
                nc.gpsimd.tensor_copy(i2[n * BLK:(n + 1) * BLK, :], ident[0:BLK, 0:BLK]).then_inc(consts_set, 1)
                pool.wait_ge(consts_set, 4 + n)
            zero(2)
            zero(3)
            pool.wait_ge(wf_hi, 1)
            nc.gpsimd.tensor_tensor(wfl[:, :, :], wf, wfh[:, :, :].bitcast(F32), ALU.subtract).then_inc(wf_lo, 1)
            pool.wait_ge(xh_ready, Q)
            pool.wait_ge(rw_in, 16)
            nc.gpsimd.tensor_tensor(x_sb[:, :, :], x_sb[:, :, :], rw[:, 1:2, :].broadcast_to([P, B, D]),
                                    ALU.add).then_inc(xb_ready, 1)
            def exp_rest(u):
                c, hf = place_of(u)
                pool.wait_ge(p_hi, u + 1)
                heads = slice(hf * GL * HG, (hf + 1) * GL * HG)
                ih, i0 = divmod(CI * c, TI)
                hi = ph[:, ih, heads, :, i0:i0 + CI].rearrange("p h b i -> p (h b) i")
                lo = pl[:, ih, heads, :, i0:i0 + CI].rearrange("p h b i -> p (h b) i")
                nc.gpsimd.tensor_tensor(lo, p32[:, u % 2, :].rearrange("p (n i) -> p n i", i=CI), hi,
                                        ALU.subtract).then_inc(p_lo, 1)

            def hidden(k):
                pool.wait_ge(gu_ready, k + 1)
                pool.wait_ge(cwr_ready, n_routed(k))
                if k >= 3:
                    pool.wait_ge(y_tile, GN * (k - 2))
                nc.gpsimd.tensor_tensor(hh[:, k % 3, :], gu[:, k % 3, :], cwr[:, k % 3, :], ALU.mult).then_inc(hid_ready, 1)

            for stage, n in POOL_STEPS:
                if stage == "shift":
                    exp_rest(n)
                elif stage == "attn":
                    power(norm_no(stage, n), n)
                elif stage == "mix":
                    power(norm_no(stage, n), n)
                elif stage == "y":
                    power(norm_no(stage, n), n)
                elif stage == "pv":
                    pool.wait_ge(ctxu_ready, n + 1)
                    nc.gpsimd.tensor_tensor(ctxv[:, n], ctxv[:, n], rec[:, n, :].rearrange("p (h o) -> p h o", o=1)
                                            .broadcast_to([P, H, DH]), ALU.mult).then_inc(ctxv_ready, 1)
                elif stage == "rest":
                    toks = slice(n * QN * T, (n + 1) * QN * T)
                    pool.wait_ge(x2T_ready, n + 1)
                    nc.gpsimd.tensor_tensor(x2l[:, toks], x2T[:, toks], x2h[:, toks].bitcast(F32),
                                            ALU.subtract).then_inc(x2l_ready, 1)
                elif stage == "hidden" and routed(n):
                    hidden(n)

        @block.scalar
        def _(act):
            act.dma_start(cl[:, :], cols).then_inc(cl_in, 16)
            act.dma_start(pe_sb[:, :], pos_emb).then_inc(pe_in, 16)
            act.dma_start(wp[:, :, :], w_proj.rearrange("p (n c) -> p n c", n=5)).then_inc(wp_in, 16)

            def split_hi(dst, src, bias=0.0):
                return nc.scalar.activation(dst, src, ACT.Identity, bias=bias)

            act.wait_ge(warm_set, 1)
            nc.scalar.activation(nm[:, 0, 0:1], i_warm[:, 0:1], ACT.Exp).then_inc(act_warm, 1)
            act.wait_ge(cl_in, 16)
            for q in range(Q):
                act.wait_ge(xT_ps, q + 1)
                batches = slice(q % 2 * GN, (q % 2 + 1) * GN)
                nc.scalar.activation(xnT_i[:, batches, q // 2, :],
                                     ps[:, (0, 1, 7, 4)[q], 0:QN * T].rearrange("p (b i) -> p b i", i=TI), ACT.Identity,
                                     bias=cl[:, 5:6], scale=cl[:, 4:5]).then_inc(xnT_ready, 1)
                if q == 1:
                    act.wait_ge(p_ps, 1)
                    split_hi(kp_c[:, 0, B * T:KPT], ps[:, 2, 0:POS]).then_inc(kp_hi, 1)

            def q_heads(ih):
                act.wait_ge(q_ps, ih + 1)
                for s in range(2):
                    split_hi(q_c[:, 0, ih, s, :], ps[:, 5 + ih, :], qb[:, s:s + 1]).then_inc(q_hi, 1)

            act.wait_ge(qb_ready, 2)
            q_heads(0)
            for g in range(G):
                act.wait_ge(k_ps, g + 1)
                split_hi(kp_c[:, 0, g * GT:(g + 1) * GT], ps[:, (3, 4)[g], :], cl[:, 1:2]).then_inc(kp_hi, 1)
            q_heads(1)
            act.wait_ge(wf_in, 16)
            nc.scalar.activation(wfh[:, :, :], wf, ACT.Copy).then_inc(wf_hi, 1)
            for g in range(G):
                act.wait_ge(v_sum, g + 1)
                split_hi(vp[:, g * GN:(g + 1) * GN, :, 0:DH].rearrange("p b h d -> p (b h) d"),
                         v32[:, g * GN:(g + 1) * GN, :].rearrange("p b (h d) -> p (b h) d", d=DH)).then_inc(v_hi, 1)

            read_q(act, 0, slice(0, GL), q_in[0])

            def exps(u):
                c, hf = place_of(u)
                act.wait_ge(shifted, u + 1)
                if u == 0:
                    act.wait_ge(wf_lo, 1)
                    for s in q_out:
                        act.wait_ge(s, 32)
                if u >= 2:
                    act.wait_ge(p_lo, u - 1)
                nc.scalar.activation(p32[:, u % 2, :].rearrange("p (k n) -> p k n", k=2), unit(u), ACT.Exp,
                                     scale=SC).then_inc(p_f32, 1)
                heads = slice(hf * GL * HG, (hf + 1) * GL * HG)
                ih, i0 = divmod(CI * c, TI)
                nc.scalar.activation(ph[:, ih, heads, :, i0:i0 + CI].rearrange("p h b i -> p (h b) i"),
                                     unit(u).rearrange("p k (n i) -> p (k n) i", i=CI), ACT.Exp,
                                     scale=SC).then_inc(p_hi, 1)

            def evacuate(dst, q, ready, done, parts=P):
                act.wait_ge(ready, q + 1)
                nc.scalar.copy(dst[0:parts, q * QN:(q + 1) * QN, :],
                               ps[0:parts, mid(q), 0:QN * T].rearrange("p (b t) -> p b t", b=QN)).then_inc(done, 1)

            for stage, n in ACT_STEPS:
                toks = slice(n * QN * T, (n + 1) * QN * T)
                if stage == "shift":
                    exps(n)
                elif stage == "ctxT":
                    evacuate(ctxT, n, ctxT_ps, ctxT_ready)
                elif stage == "norm":
                    evacuate(x1T, n, x1T_ps, x1T_ready)
                elif stage == "cross":
                    act.wait_ge(nm2_ready, n + 1)
                    for j in range(QN):
                        b = n * QN + j
                        nc.scalar.activation(p2[:, b, :], ps[:, mid(n), j * S:(j + 1) * S], ACT.Exp,
                                             bias=r8[:, 0, b:b + 1], accum_out=r8[:, 1, b:b + 1]).then_inc(p2_ready, 1)
                elif stage == "probs":
                    evacuate(p2T, n, p2T_ps, p2T_ready, parts=S)
                elif stage == "next":
                    act.wait_ge(x2T_ps, n + 1)
                    nc.scalar.activation(x2h[:, toks], ps[:, mid(n), 0:QN * T], ACT.Copy).then_inc(x2h_ready, 1)
                    nc.scalar.copy(x2T[:, toks], ps[:, mid(n), 0:QN * T]).then_inc(x2T_ready, 1)
                elif stage == "router":
                    act.wait_ge(lg_ready, n + 1)
                    nc.scalar.activation(pr[:, n * GN:(n + 1) * GN], pr[:, n * GN:(n + 1) * GN], ACT.Exp).then_inc(pr_ready, 1)
                elif stage == "gate_up":
                    act.wait_ge(gate_ps, n + 1)
                    if n >= 3:
                        act.wait_ge(ga_ready, n - 2)
                    nc.scalar.activation(th[:, n % 3, :], ps[:, n % 2, :], ACT.Tanh, scale=0.5).then_inc(th_ready, 1)
                elif stage == "cwT":
                    act.wait_ge(cwT_ps, n + 1)
                    nc.scalar.copy(cwT[0:E, n * GT:(n + 1) * GT], ps[0:E, 7, :]).then_inc(cwT_hi, 1)
                elif stage == "cwr" and routed(n):
                    act.wait_ge(cwr_ps, n_routed(n))
                    if n >= 4:
                        act.wait_ge(hid_ready, n - 2)
                    nc.scalar.copy(cwr[:, n % 3, :], ps[:, CW_BANK, :]).then_inc(cwr_ready, 1)

        @block.vector
        def _(dve):
            nc.vector.memset(i_warm[:, :], 1.0).then_inc(warm_set, 1)
            steps = [0]

            def link(ins):
                steps[0] += 1
                ins.then_inc(dve_step, 1)
                dve.wait_ge(dve_step, steps[0])

            def quarter(v, q):
                return v[:, q * QN:(q + 1) * QN]

            def group(v, g):
                return v[:, g * GN:(g + 1) * GN]

            def stats(src, q):
                for b in range(q * QN, (q + 1) * QN):
                    last = nc.vector.bn_stats(st[:, b, :], src[:, b, :])
                link(last)
                for b in range(q * QN, (q + 1) * QN):
                    last = nc.vector.bn_aggr(mv[:, b, :], st[:, b, :])
                link(last)
                nc.vector.tensor_scalar_add(quarter(ve, q), quarter(mv, q)[:, :, 1], EPS).then_inc(var_ready, 1)

            def norm(n, q, dst, src, ready):
                dve.wait_ge(rstd_ready, n + 1)
                for b in range(q * QN, (q + 1) * QN):
                    last = nc.vector.tensor_scalar(dst[:, b, :], src[:, b, :], mv[:, b, 0:1], rstd[:, b:b + 1],
                                                   ALU.subtract, ALU.mult)
                last.then_inc(ready, 1)

            for q in range(Q):
                dve.wait_ge(x_in[q // 2], 16)
                stats(x_sb, q)
                if q:
                    norm(q - 1, q - 1, xh, x_sb, xh_ready)
            norm(Q - 1, Q - 1, xh, x_sb, xh_ready)
            dve.wait_ge(cl_in, 16)
            for s in range(2):
                nc.vector.tensor_tensor(qb[:, s:s + 1], cl[:, 0:1], cl[:, 2 + s:3 + s], ALU.add).then_inc(qb_ready, 1)

            dve.wait_ge(kp_hi, 1)
            nc.vector.tensor_tensor(kp_c[:, 1, B * T:KPT], ps[:, 2, 0:POS], kp_c[:, 0, B * T:KPT],
                                    ALU.subtract).then_inc(kp_lo, 1)
            def q_rests(ih):
                dve.wait_ge(q_hi, 2 * ih + 2)
                for s in range(2):
                    nc.vector.scalar_tensor_tensor(out=q_c[:, 1, ih, s, :], in0=ps[:, 5 + ih, :],
                                                   scalar=qb[:, s:s + 1], in1=q_c[:, 0, ih, s, :],
                                                   op0=ALU.add, op1=ALU.subtract).then_inc(q_lo, 1)

            dve.wait_ge(qb_ready, 2)
            q_rests(0)
            for g in range(G):
                cols_g = slice(g * GT, (g + 1) * GT)
                dve.wait_ge(kp_hi, 2 + g)
                nc.vector.scalar_tensor_tensor(out=kp_c[:, 1, cols_g], in0=ps[:, (3, 4)[g], :], scalar=cl[:, 1:2],
                                               in1=kp_c[:, 0, cols_g], op0=ALU.add, op1=ALU.subtract).then_inc(kp_lo, 1)
            q_rests(1)
            dve.wait_ge(rw_in, 16)
            for g in range(G):
                dve.wait_ge(v_ps, g + 1)
                nc.vector.tensor_tensor(group(v32, g), ps[:, (7, 2)[g], :].rearrange("p (b c) -> p b c", b=GN),
                                        rw[:, 0:1, :].broadcast_to([P, GN, D]), ALU.add).then_inc(v_sum, 1)
            for g in range(G):
                dve.wait_ge(v_hi, g + 1)
                nc.vector.tensor_tensor(group(vp, g)[:, :, :, DH:2 * DH].rearrange("p b h d -> p (b h) d"),
                                        group(v32, g).rearrange("p b (h d) -> p (b h) d", d=DH),
                                        group(vp, g)[:, :, :, 0:DH].rearrange("p b h d -> p (b h) d"),
                                        ALU.subtract).then_inc(v_lo, 1)

            dve.wait_ge(consts_set, 5)

            def maxima(u):
                m = u % 2
                dve.wait_ge(scores, u + 1)
                link(nc.vector.tensor_reduce(pm[:, m, 0, :], unit(u).rearrange("p k (n c) -> p (k n) c", c=BLK), AX,
                                             ALU.max, apply_transpose=True))
                for q in range(1, 4):
                    last = nc.vector.tensor_copy(pm[0:BLK, m, q, :], pm[BLK * q:BLK * (q + 1), m, 0, :])
                link(last)
                link(nc.vector.tensor_reduce(nmx[:, m, :], pm[0:BLK, m, :, :].rearrange("p q n -> p n q"), AX,
                                             ALU.max, negate=True))
                if u >= 2:
                    dve.wait_ge(shifted, u - 1)
                link(nc.vector.tensor_copy(nm[0:BLK, m, :], nmx[:, m, :]))
                nc.vector.tensor_tensor(nm[BLK:2 * BLK, m, :], nmx[:, m, :], nm[0:BLK, m, :],
                                        ALU.subtract).then_inc(shift_ready, 1)

            def attention_out(t):
                dve.wait_ge(pv_ps, t + 1)
                heads = ps[:, pv_bank(t):pv_bank(t) + 2, :].rearrange("p k (h w) -> p (k h) w", w=HW)
                for bl in range(2):
                    mine = heads[rows_of(bl), :, bl * VW:(bl + 1) * VW]
                    nc.vector.reciprocal(rec[rows_of(bl), t, :], mine[:, :, VW - 1])
                    last = nc.vector.tensor_reduce(ctxv[rows_of(bl), t],
                                                   mine[:, :, 0:2 * DH].rearrange("p h (k d) -> p h d k", k=2), AX, ALU.add)
                last.then_inc(ctxu_ready, 1)

            def spread(v, g):
                return r8[:, v, g * GN:(g + 1) * GN].rearrange("p (b o) -> p b o", o=1).broadcast_to([P, GN, E])

            def scalar_of(v, g):
                return r8[:, v, g * GN:(g + 1) * GN]

            def pick(g):
                dve.wait_ge(pr_ready, g + 1)
                p_g, key_g, s1_g, s2_g, tie_g, cw_g = (group(v, g) for v in (pr, key, s1, s2, tie, cw))
                nc.vector.tensor_reduce(scalar_of(4, g), p_g, AX, ALU.add)
                link(nc.vector.tensor_reduce(scalar_of(5, g), p_g, AX, ALU.max))
                nc.vector.reciprocal(scalar_of(6, g), scalar_of(4, g))
                link(nc.vector.tensor_tensor(key_g, p_g, spread(5, g), ALU.is_equal))
                nc.vector.tensor_tensor(cw_g, p_g, spread(6, g), ALU.mult)
                link(nc.vector.tensor_tensor(key_g, key_g, tie_g, ALU.mult))
                link(nc.vector.tensor_reduce(scalar_of(7, g), key_g, AX, ALU.max))
                link(nc.vector.tensor_tensor(s1_g, key_g, spread(7, g), ALU.is_equal))
                link(nc.vector.scalar_tensor_tensor(out=s2_g, in0=s1_g, scalar=-BIG, in1=p_g, op0=ALU.mult, op1=ALU.add))
                link(nc.vector.tensor_reduce(scalar_of(8, g), s2_g, AX, ALU.max))
                link(nc.vector.tensor_tensor(key_g, s2_g, spread(8, g), ALU.is_equal))
                link(nc.vector.tensor_tensor(key_g, key_g, tie_g, ALU.mult))
                link(nc.vector.tensor_reduce(scalar_of(9, g), key_g, AX, ALU.max))
                link(nc.vector.tensor_tensor(s2_g, key_g, spread(9, g), ALU.is_equal))
                link(nc.vector.tensor_tensor(s1_g, s1_g, s2_g, ALU.add))
                nc.vector.tensor_tensor(cw_g, s1_g, cw_g, ALU.mult).then_inc(cw_ready, 1)

            def hidden(k):
                m = k % 3
                dve.wait_ge(th_ready, k + 1)
                nc.vector.scalar_tensor_tensor(out=ga[:, m, :], in0=th[:, m, :], scalar=1.0, in1=ps[:, k % 2, :],
                                               op0=ALU.add, op1=ALU.mult).then_inc(ga_ready, 1)
                dve.wait_ge(ga_ready, k + 1)
                dve.wait_ge(up_ps, k + 1)
                if k >= 3:
                    dve.wait_ge(hid_ready, k - 2)
                nc.vector.tensor_tensor(gu[:, m, :], ga[:, m, :], ps[:, 2 + k % 2, :], ALU.mult).then_inc(gu_ready, 1)
                if not routed(k):
                    dve.wait_ge(gu_ready, k + 1)
                    if k >= 3:
                        dve.wait_ge(y_tile, GN * (k - 2))
                        dve.wait_ge(hid_ready, k)
                    nc.vector.tensor_scalar(hh[:, m, :], gu[:, m, :], 0.5, None, ALU.mult).then_inc(hid_ready, 1)

            for stage, n in DVE_STEPS:
                if stage == "scores":
                    maxima(n)
                elif stage == "pv":
                    attention_out(n)
                elif stage == "attn":
                    dve.wait_ge(xb_ready, 1)
                    dve.wait_ge(y1_ps, n + 1)
                    nc.vector.tensor_tensor(quarter(z, n), ps[:, mid(n), 0:QN * D].rearrange("p (b c) -> p b c", b=QN),
                                            quarter(x_sb, n), ALU.add).then_inc(z_ready, 1)
                    dve.wait_ge(z_ready, norm_no(stage, n) - Q + 1)
                    stats(z, n)
                elif stage == "norm":
                    norm(norm_no("attn", n), n, x1, z, x1_ready)
                elif stage == "cross":
                    dve.wait_ge(s2_ps, n + 1)
                    nc.vector.tensor_reduce(r8[:, 0, n * QN:(n + 1) * QN],
                                            ps[:, mid(n), 0:QN * S].rearrange("p (b s) -> p b s", b=QN), AX, ALU.max,
                                            negate=True).then_inc(nm2_ready, 1)
                elif stage == "mix":
                    dve.wait_ge(o2_ps, n + 1)
                    link(nc.vector.reciprocal(r8[:, 2, n * QN:(n + 1) * QN], r8[:, 1, n * QN:(n + 1) * QN]))
                    for j in range(QN):
                        b = n * QN + j
                        last = nc.vector.scalar_tensor_tensor(out=z[:, b, :], in0=ps[:, mid(n), j * D:(j + 1) * D],
                                                              scalar=r8[:, 2, b:b + 1], in1=x1[:, b, :],
                                                              op0=ALU.mult, op1=ALU.add)
                    last.then_inc(z_ready, 1)
                    dve.wait_ge(z_ready, norm_no(stage, n) - Q + 1)
                    stats(z, n)
                elif stage == "next":
                    norm(norm_no("mix", n), n, x2, z, x2_ready)
                elif stage == "router":
                    dve.wait_ge(lg_ps, 2 * n + 2)
                    for q in (2 * n, 2 * n + 1):
                        logits = ps[:, mid(q), 0:QN * E].rearrange("p (b e) -> p b e", b=QN)
                        link(nc.vector.tensor_reduce(r8[:, 3, q * QN:(q + 1) * QN], logits, AX, ALU.max))
                        last = nc.vector.tensor_tensor(quarter(pr, q), logits,
                                                       r8[:, 3, q * QN:(q + 1) * QN].rearrange("p (b o) -> p b o", o=1)
                                                       .broadcast_to([P, QN, E]), ALU.subtract)
                    last.then_inc(lg_ready, 1)
                elif stage == "pick":
                    dve.wait_ge(moe_in, 48)
                    pick(n)
                elif stage == "cwT":
                    dve.wait_ge(cwT_hi, n + 1)
                    nc.vector.tensor_tensor(cwT[32:32 + E, n * GT:(n + 1) * GT], ps[0:E, 7, :],
                                            cwT[0:E, n * GT:(n + 1) * GT], ALU.subtract).then_inc(cwT_ready, 1)
                elif stage == "hidden":
                    hidden(n)
                elif stage == "y":
                    dve.wait_ge(y_tile, GN * (HID * (n // 2 + 1) - 1) + (QN if n == 2 else GN))
                    bank, col = y_place(n * QN)
                    nc.vector.tensor_tensor(quarter(z, n), ps[:, bank, col:col + QN * D]
                                            .rearrange("p (b c) -> p b c", b=QN), quarter(x2, n),
                                            ALU.add).then_inc(z_ready, 1)
                    dve.wait_ge(z_ready, norm_no(stage, n) - Q + 1)
                    stats(z, n)
                elif stage == "o":
                    norm(norm_no("y", n), n, o_sb, z, o_ready)

        @block.tensor
        def _(pe):
            def mm(o, w, r, start, stop):
                return nc.tensor.matmul(o, w, r, start=start, stop=stop, skip_group_check=True)

            pe.wait_ge(warm_set, 1)
            for n in range(12):
                mm(ps[:, 6, :], i_warm[:, 0:P], i_warm[:, :], True, True)
            pe.wait_ge(id_in, 16)
            for q in range(Q):
                pe.wait_ge(xh_ready, q + 1)
                for j in range(QN):
                    last = nc.tensor.transpose(ps[:, (0, 1, 7, 4)[q], j * T:(j + 1) * T], xh[:, q * QN + j, :], ident[:, :])
                last.then_inc(xT_ps, 1)
                if q == 1:
                    pe.wait_ge(pe_in, 16)
                    pe.wait_ge(wp_in, 16)
                    mm(ps[:, 2, 0:POS], wp[:, 2, :], pe_sb[:, :], True, True).then_inc(p_ps, 1)
                if q == 3:
                    pe.wait_ge(xnT_ready, 2)
                    mm(ps[:, 5, :], wp[:, 0, :], xnT_i[:, :, 0, :], True, True).then_inc(q_ps, 1)
            for g in range(G):
                pe.wait_ge(xnT_ready, 3 + g)
                mm(ps[:, (3, 4)[g], :], wp[:, 1, :], xnT[:, g * GT:(g + 1) * GT], True, True).then_inc(k_ps, 1)
            mm(ps[:, 6, :], wp[:, 0, :], xnT_i[:, :, 1, :], True, True).then_inc(q_ps, 1)
            pe.wait_ge(kp_lo, 1)
            for g in range(G):
                for j in range(GN):
                    b = g * GN + j
                    last = mm(ps[:, (7, 2)[g], j * D:(j + 1) * D], xnT[:, b * T:(b + 1) * T], wp[:, 3, :], j == 0, True)
                last.then_inc(v_ps, 1)

            def unit_scores(u):
                c, hf = place_of(u)
                ih, i0 = divmod(CI * c, TI)
                for k in range(GL):
                    g = GL * hf + k
                    bank = unit(u)[:, k, :].rearrange("p (h b i) -> p h b i", h=HG, b=B)
                    for b in range(B):
                        mm(bank[:, :, b, :], kp[:, g, b * T:(b + 1) * T], qd[:, ih, :, g, 0, b, i0:i0 + CI],
                           b == 0, False)
                    for i in range(i0, i0 + CI):
                        a = B * T + T - 1 - (ih * TI + i)
                        last = mm(bank[:, :, :, i - i0], kp[:, g, a:a + T], qd[:, ih, :, g, 1, :, i], False, False)
                last.then_inc(scores, 1)

            def unit_shift(u):
                pe.wait_ge(shift_ready, u + 1)
                for n in range(NBLK):
                    last = mm(unit(u)[:, n // 16, (n % 16) * BLK:(n % 16 + 1) * BLK],
                              nm[:, u % 2, n:n + 1].to_broadcast([P, P]), i2[:, :], False, True)
                last.then_inc(shifted, 1)

            for n in range(36):
                mm(ps[:, 0, :], i_warm[:, 0:P], i_warm[:, :], True, True)
            pe.wait_ge(consts_set, 5)
            def transposes(q, src, ready, count, done, parts=P):
                pe.wait_ge(ready, count)
                for j in range(QN):
                    last = nc.tensor.transpose(ps[0:parts, mid(q), j * T:(j + 1) * T], src(q * QN + j), ident[:, :])
                last.then_inc(done, 1)

            def products(q, width, pair, done):
                for j in range(QN):
                    w, r = pair(q * QN + j)
                    last = mm(ps[:, mid(q), j * width:(j + 1) * width], w, r, j == 0, True)
                last.then_inc(done, 1)

            def half_products(q, width, pair, done):
                for j in range(QN):
                    for bl in range(2):
                        w, r = pair(q * QN + j, bl)
                        last = mm(ps[rows_of(bl), mid(q), j * width:(j + 1) * width], w, r, j == 0, True)
                last.then_inc(done, 1)

            def attention(t):
                bs = slice(batch_of(t, 0), batch_of(t, 1) + 1)
                ih = t // TM
                for h in range(H):
                    m = (h % NG) * HG + h // NG
                    bank, col = pv_bank(t) + h // (H // 2), h % (H // 2) * HW
                    o = ps[:, bank, col:col + 2 * VW]
                    mm(o, ph[:, ih, m, bs, :].rearrange("p b i -> p (b i)"), vp[:, bs, h, :], col == 0, False)
                    last = mm(o, pl[:, ih, m, bs, :].rearrange("p b i -> p (b i)"), vp[:, bs, h, :], False, True)
                last.then_inc(pv_ps, 1)

            def tile_of(k):
                return k % HID - 1 if routed(k) else SHARED

            def tokens(k):
                return slice(k // HID * GT, (k // HID + 1) * GT)

            def gate_up(k):
                if k == 0:
                    pe.wait_ge(ctxu_ready, 2 * TM)
                if k % HID == 0:
                    pe.wait_ge(wf_lo, 1)
                    pe.wait_ge(x2l_ready, Q // 2 * (k // HID + 1))
                for part, bank, read, done in ((0, k % 2, ga_ready, gate_ps), (1, 2 + k % 2, gu_ready, up_ps)):
                    if k >= 2:
                        pe.wait_ge(read, k - 1)
                    w = 2 * tile_of(k) + part
                    mm(ps[:, bank, :], wfh[:, w, :], x2l[:, tokens(k)], True, False)
                    mm(ps[:, bank, :], wfl[:, w, :], x2h[:, tokens(k)], False, False)
                    mm(ps[:, bank, :], wfh[:, w, :], x2h[:, tokens(k)], False, True).then_inc(done, 1)

            read_by = {"ctxT": lambda q: (ctxT_ready, q + 1), "attn": lambda q: (z_ready, norm_no("attn", q) - Q + 1),
                       "norm": lambda q: (x1T_ready, q + 1), "cross": lambda q: (p2_ready, QN * (q + 1)),
                       "probs": lambda q: (p2T_ready, q + 1), "mix": lambda q: (z_ready, norm_no("mix", q) - Q + 1),
                       "next": lambda q: (x2T_ready, q + 1), "lg": lambda q: (lg_ready, q // 2 + 1)}
            reader = {bank: None for bank in range(8)}

            for stage, n in PE_STEPS:
                if stage == "pv":
                    for bank in (pv_bank(n), pv_bank(n) + 1):
                        if reader[bank]:
                            pe.wait_ge(*reader[bank])
                        reader[bank] = (ctxu_ready, n + 1)
                elif stage in read_by or stage == "cwT":
                    bank = 7 if stage == "cwT" else mid(n)
                    if reader[bank]:
                        pe.wait_ge(*reader[bank])
                    reader[bank] = (cwT_ready, n + 1) if stage == "cwT" else read_by[stage](n)
                if stage == "warm":
                    pe.wait_ge(p_hi, UNITS - 1)
                    for _ in range(n):
                        mm(ps[:, WARM_BANK, :], i_warm[:, 0:P], i_warm[:, :], True, True)
                elif stage == "scores":
                    if n in (0, 2):
                        pe.wait_ge(kp_in[n // 2], 16)
                        pe.wait_ge(q_in[n // 2], 16 * HG)
                    if n == UH:
                        pe.wait_ge(q_in[2], 16 * HG)
                    if n == 1:
                        pe.wait_ge(v_sum, G)
                    if n >= SLOTS:
                        pe.wait_ge(p_hi, n - SLOTS + 1)
                    unit_scores(n)
                elif stage == "shift":
                    unit_shift(n)
                elif stage == "pv":
                    if n % TM == 0:
                        pe.wait_ge(v_lo, G)
                        pe.wait_ge(p_lo, UH * (n // TM + 1))
                    attention(n)
                elif stage == "ctxT":
                    transposes(n, lambda b: ctxv[:, b].rearrange("p h d -> p (h d)"), ctxv_ready, QN * (n + 1), ctxT_ps)
                elif stage == "attn":
                    pe.wait_ge(ctxT_ready, n + 1)
                    products(n, D, lambda b: (ctxT[:, b, :], wp[:, 4, :]), y1_ps)
                elif stage == "norm":
                    transposes(n, lambda b: x1[:, b, :], x1_ready, n + 1, x1T_ps)
                elif stage == "cross":
                    pe.wait_ge(ctx_in, 32)
                    pe.wait_ge(x1T_ready, n + 1)
                    half_products(n, S, lambda t, bl: (x1T[:, t, rows_of(bl)], ct[:, batch_of(t, bl), :]), s2_ps)
                elif stage == "probs":
                    transposes(n, lambda b: p2[:, b, :], p2_ready, QN * (n + 1), p2T_ps, parts=S)
                elif stage == "mix":
                    pe.wait_ge(p2T_ready, n + 1)
                    half_products(n, D, lambda t, bl: (p2T[0:S, t, rows_of(bl)], cn[0:S, batch_of(t, bl), :]), o2_ps)
                elif stage == "next":
                    transposes(n, lambda b: x2[:, b, :], x2_ready, n + 1, x2T_ps)
                elif stage == "lg":
                    pe.wait_ge(wr_in, 16)
                    pe.wait_ge(x2T_ready, n + 1)
                    products(n, E, lambda b: (x2T[:, b * T:(b + 1) * T], wr[:, :]), lg_ps)
                elif stage == "gate_up":
                    gate_up(n)
                elif stage == "cwT":
                    pe.wait_ge(cw_ready, n + 1)
                    for j in range(GN):
                        last = nc.tensor.transpose(ps[0:E, 7, j * T:(j + 1) * T], cw[:, n * GN + j, :], ident[:, :])
                    last.then_inc(cwT_ps, 1)
                elif stage == "cwr" and routed(n):
                    pe.wait_ge(cwT_ready, n // HID + 1)
                    if n_routed(n) >= 2:
                        pe.wait_ge(cwr_ready, n_routed(n) - 1)
                    mm(ps[:, CW_BANK, :], sel[0:64, tile_of(n), :], cwT[0:64, tokens(n)], True, True).then_inc(cwr_ps, 1)
                elif stage == "down":
                    pe.wait_ge(moe_in, 48)
                    pe.wait_ge(hid_ready, n + 1)
                    for j in range(GN):
                        bank, col = y_place(n // HID * GN + j)
                        mm(ps[:, bank, col:col + D], hh[:, n % 3, j * T:(j + 1) * T], wd[:, tile_of(n), :],
                           not routed(n) and col == 0, n % HID == HID - 1).then_inc(y_tile, 1)


def kernel(**inputs):
    import math
    import numpy as np
    import concourse.bacc as bacc
    from concourse.bass_utils import run_bass_kernel_spmd

    def a(name):
        return np.asarray(inputs[name])

    def grouped(w):
        return w.reshape((HG, NG, DH, -1)).transpose(0, 2, 1, 3).reshape(w.shape)

    L = "L0_attn_"
    w_proj = np.concatenate([grouped(a(L + "Wq")).T, grouped(a(L + "Wk")).T, grouped(a(L + "Wpos")).T,
                             a(L + "Wv").T, a(L + "Wout").T], axis=1)
    cols = np.stack([grouped(a(L + "bq")), grouped(a(L + "bk")), grouped(a(L + "u_bias").reshape(D)),
                     grouped(a(L + "v_bias").reshape(D)), a(L + "ln_gamma"), a(L + "ln_beta")], axis=1)
    rows = np.stack([a(L + "bv"), a(L + "bout")])[None]
    wg = a("L0_ffn_Wg").transpose(1, 0, 2).reshape(D, PAIRS, 2 * F)
    wu = a("L0_ffn_Wu").transpose(1, 0, 2).reshape(D, PAIRS, 2 * F)
    gate = np.concatenate([wg, a("L0_ffn_Sg")[:, None]], axis=1)
    upw = np.concatenate([wu, a("L0_ffn_Su")[:, None]], axis=1)
    w_ffn = np.stack([gate, upw], axis=2).reshape(D, 2 * HID * P)
    wdn = np.concatenate([a("L0_ffn_Wd").reshape(PAIRS, 2 * F, D), a("L0_ffn_Sd")[None]], axis=0)
    w_down = wdn.transpose(1, 0, 2).reshape(P, HID * D)
    ctx = a("ctx_1024")

    dist = (T - 1 - np.arange(2 * T - 1)).astype(np.float32)
    div = np.exp(np.arange(0, D, 2, dtype=np.float32) * np.float32(-math.log(10000.0) / D))
    ang = np.abs(dist)[:, None] * div * np.sign(dist)[:, None]
    pos = np.zeros((D, POS), np.float32)
    pos[0::2, :2 * T - 1] = np.sin(ang).T
    pos[1::2, :2 * T - 1] = np.cos(ang).T
    sel = np.zeros((64, PAIRS, P), np.float16)
    for e in range(E):
        for base in (0, 32):
            sel[base + e, e // 2, (e % 2) * F:(e % 2 + 1) * F] = 0.5
    tie = np.tile((E - np.arange(E)).astype(np.float32), (1, B, 1))

    data = {
        "x": a("x").reshape(TM, 2, IH, TI, D).transpose(1, 3, 2, 0, 4).reshape(P, B, D), "ctx_n": ctx, "ctx_t": ctx.transpose(2, 0, 1).reshape(D, B * S), "w_proj": w_proj,
        "w_r": a("L0_ffn_Wr"), "w_ffn": w_ffn, "w_down": w_down, "cols": cols, "rows": rows, "pos_emb": pos,
        "ident_d": np.eye(P, dtype=np.float32), "sel_d": sel, "tie_d": tie,
    }
    nc = bacc.Bacc("TRN2", target_bir_lowering=False, num_devices=1)
    arrays, args = {}, []
    for name, value in data.items():
        value = np.ascontiguousarray(value)
        arrays[f"in_{name}"] = value
        args.append(nc.dram_tensor(f"in_{name}", value.shape, mybir.dt.from_np(value.dtype), kind="ExternalInput").ap())
    out = nc.dram_tensor("out_0", (P, B, D), F32, kind="ExternalOutput").ap()
    decoder_block(nc, *args, out)
    r = run_bass_kernel_spmd(nc, [arrays], core_ids=[0])
    return r.results[0]["out_0"].reshape(2, TI, IH, TM, D).transpose(3, 0, 2, 1, 4).reshape(B, T, D)
```
